# Optimizing a Trainium2 kernel written in Bass

```python
import numpy as np
import jax
import jax.numpy as jnp

def _softmax(x, axis=-1):
    return jax.nn.softmax(x, axis=axis)

def _gelu(x):
    return jax.nn.gelu(x, approximate=True)

def _silu(x):
    return jax.nn.silu(x)

def _sigmoid(x):
    return jax.nn.sigmoid(x)

def _layernorm(x, axis=-1, eps=1e-05):
    m = jnp.mean(x, axis=axis, keepdims=True)
    v = jnp.var(x, axis=axis, keepdims=True)
    return (x - m) / jnp.sqrt(v + eps)

def _scatter_add(tgt, idx, src, axis=0):
    return tgt.at[idx].add(src)

def _segment_sum(src, seg, n):
    return jax.ops.segment_sum(src, seg, n)
kernel_name = 'mk_perceiver_d1_seqx_r2_40a6de'

def setup_inputs(seed: int=0):
    np.random.seed(seed)
    _w = jnp.asarray

    def _rec_inputs():
        import jax
        import jax.numpy as jnp
        _rk = jax.random.key(seed)
        x = -0.0002928 + 1 * jax.random.normal(jax.random.fold_in(_rk, 1), (4, 128, 512), jnp.float32)
        _lenS = 128 - jax.random.randint(jax.random.fold_in(_rk, 7), (4,), 0, max(1, 128 // 4) + 1, jnp.int32)
        _lenS2 = 2048 - jax.random.randint(jax.random.fold_in(_rk, 8), (4,), 0, max(1, 2048 // 4) + 1, jnp.int32)
        _ctx_1024P = jax.random.normal(jax.random.fold_in(_rk, 11), (4, 16, 512), jnp.float32)
        _ctx_1024c = jax.random.dirichlet(jax.random.fold_in(_rk, 511), 0.3 * jnp.ones((16,), jnp.float32), (4, 2048))
        _ctx_1024t = jnp.einsum('bsk,bkd->bsd', _ctx_1024c, _ctx_1024P)
        _ctx_1024t = _ctx_1024t * jax.lax.rsqrt(jnp.mean(jnp.square(_ctx_1024t)) + 1e-12) * 0.953939
        ctx_1024 = -1.39393e-06 + 0.999914 * (_ctx_1024t + 0.3 * jax.random.normal(jax.random.fold_in(_rk, 611), (4, 2048, 512), jnp.float32))
        return (x, ctx_1024)
    x, ctx_1024 = _rec_inputs()

    def _L0_xattn_setup():
        import jax, jax.numpy as jnp
        import numpy as np
        B, S, D, H = (2, 1024, 512, 16)
        DK = D // H
        key = jax.random.key(seed)
        ks = jax.random.split(key, 11)
        s = 1.0 / np.sqrt(D)
        w = lambda k: jax.random.normal(k, (D, D), jnp.float32) * s
        b = lambda k: jax.random.normal(k, (D,), jnp.float32) * s
        return {'query': jax.random.normal(ks[0], (B, S, D), jnp.float32), 'key': jax.random.normal(ks[1], (B, S, D), jnp.float32), 'value': jax.random.normal(ks[2], (B, S, D), jnp.float32), 'Wq': w(ks[3]), 'bq': b(ks[4]), 'Wk': w(ks[5]), 'bk': b(ks[6]), 'Wv': w(ks[7]), 'bv': b(ks[8]), 'Wo': w(ks[9]), 'bo': b(ks[10])}
    _L0_xattn_all = _L0_xattn_setup()
    _L0_xattn_in = {k: v for k, v in _L0_xattn_all.items() if k in ('Wq', 'bq', 'Wk', 'bk', 'Wv', 'bv', 'Wo', 'bo')}
    del _L0_xattn_all

    def _L0_attn_setup():
        import jax, jax.numpy as jnp
        import numpy as np
        N_HEADS = 16
        MAX_DIST = 64
        key = jax.random.key(seed)
        ks = jax.random.split(key, 7)
        B, S, D = (16, 256, 512)
        hd = D // N_HEADS
        num_rel = 2 * MAX_DIST + 1
        s = 0.02
        return {'x': jax.random.normal(ks[0], (B, S, D), dtype=jnp.float32), 'Wq': jax.random.normal(ks[1], (D, D), dtype=jnp.float32) * s, 'Wk': jax.random.normal(ks[2], (D, D), dtype=jnp.float32) * s, 'Wv': jax.random.normal(ks[3], (D, D), dtype=jnp.float32) * s, 'Eq': jax.random.normal(ks[4], (num_rel, hd), dtype=jnp.float32) * s, 'Ek': jax.random.normal(ks[5], (num_rel, hd), dtype=jnp.float32) * s, 'Ev': jax.random.normal(ks[6], (num_rel, hd), dtype=jnp.float32) * s}
    _L0_attn_all = _L0_attn_setup()
    _L0_attn_in = {k: v for k, v in _L0_attn_all.items() if k in ('Wq', 'Wk', 'Wv', 'Eq', 'Ek', 'Ev')}
    del _L0_attn_all

    def _L0_ffn_setup():
        import jax, jax.numpy as jnp
        import numpy as np
        import math
        DIM = 512
        NUM_HEADS = 16
        SHARED_HEADS = 1
        ROUTED_HEADS = 3
        HEAD_DIM = DIM // NUM_HEADS
        B, N = (2, 1024)
        key = jax.random.key(seed)
        ks = jax.random.split(key, 16)
        s = 1.0 / math.sqrt(DIM)
        inp = {'x': jax.random.normal(ks[0], (B, N, DIM), dtype=jnp.float32), 'Wq': jax.random.uniform(ks[1], (DIM, DIM), minval=-s, maxval=s), 'bq': jax.random.uniform(ks[2], (DIM,), minval=-s, maxval=s), 'Wk': jax.random.uniform(ks[3], (DIM, DIM), minval=-s, maxval=s), 'bk': jax.random.uniform(ks[4], (DIM,), minval=-s, maxval=s), 'Wv': jax.random.uniform(ks[5], (DIM, DIM), minval=-s, maxval=s), 'bv': jax.random.uniform(ks[6], (DIM,), minval=-s, maxval=s), 'Wp': jax.random.uniform(ks[7], (DIM, DIM), minval=-s, maxval=s), 'bp': jax.random.uniform(ks[8], (DIM,), minval=-s, maxval=s), 'Wr': jax.random.uniform(ks[9], (NUM_HEADS - SHARED_HEADS, DIM), minval=-s, maxval=s), 'br': jax.random.uniform(ks[10], (NUM_HEADS - SHARED_HEADS,), minval=-s, maxval=s), 'Ws': jax.random.uniform(ks[11], (2, DIM), minval=-s, maxval=s), 'bs': jax.random.uniform(ks[12], (2,), minval=-s, maxval=s), 'temperature': jnp.full((NUM_HEADS, 1, 1), float(np.log(np.expm1(1.0 / 0.24))), dtype=jnp.float32), 'query_embedding': 0.02 * jax.random.normal(ks[13], (NUM_HEADS, 1, HEAD_DIM), dtype=jnp.float32)}
        return inp
    _L0_ffn_all = _L0_ffn_setup()
    _L0_ffn_in = {k: v for k, v in _L0_ffn_all.items() if k in ('Wq', 'bq', 'Wk', 'bk', 'Wv', 'bv', 'Wp', 'bp', 'Wr', 'br', 'Ws', 'bs', 'temperature', 'query_embedding')}
    del _L0_ffn_all
    return {'x': x, 'ctx_1024': ctx_1024, 'L0_xattn_Wq': _L0_xattn_in['Wq'], 'L0_xattn_bq': _L0_xattn_in['bq'], 'L0_xattn_Wk': _L0_xattn_in['Wk'], 'L0_xattn_bk': _L0_xattn_in['bk'], 'L0_xattn_Wv': _L0_xattn_in['Wv'], 'L0_xattn_bv': _L0_xattn_in['bv'], 'L0_xattn_Wo': _L0_xattn_in['Wo'], 'L0_xattn_bo': _L0_xattn_in['bo'], 'L0_attn_Wq': _L0_attn_in['Wq'], 'L0_attn_Wk': _L0_attn_in['Wk'], 'L0_attn_Wv': _L0_attn_in['Wv'], 'L0_attn_Eq': _L0_attn_in['Eq'], 'L0_attn_Ek': _L0_attn_in['Ek'], 'L0_attn_Ev': _L0_attn_in['Ev'], 'L0_ffn_Wq': _L0_ffn_in['Wq'], 'L0_ffn_bq': _L0_ffn_in['bq'], 'L0_ffn_Wk': _L0_ffn_in['Wk'], 'L0_ffn_bk': _L0_ffn_in['bk'], 'L0_ffn_Wv': _L0_ffn_in['Wv'], 'L0_ffn_bv': _L0_ffn_in['bv'], 'L0_ffn_Wp': _L0_ffn_in['Wp'], 'L0_ffn_bp': _L0_ffn_in['bp'], 'L0_ffn_Wr': _L0_ffn_in['Wr'], 'L0_ffn_br': _L0_ffn_in['br'], 'L0_ffn_Ws': _L0_ffn_in['Ws'], 'L0_ffn_bs': _L0_ffn_in['bs'], 'L0_ffn_temperature': _L0_ffn_in['temperature'], 'L0_ffn_query_embedding': _L0_ffn_in['query_embedding']}

def reference(x, ctx_1024, L0_xattn_Wq, L0_xattn_bq, L0_xattn_Wk, L0_xattn_bk, L0_xattn_Wv, L0_xattn_bv, L0_xattn_Wo, L0_xattn_bo, L0_attn_Wq, L0_attn_Wk, L0_attn_Wv, L0_attn_Eq, L0_attn_Ek, L0_attn_Ev, L0_ffn_Wq, L0_ffn_bq, L0_ffn_Wk, L0_ffn_bk, L0_ffn_Wv, L0_ffn_bv, L0_ffn_Wp, L0_ffn_bp, L0_ffn_Wr, L0_ffn_br, L0_ffn_Ws, L0_ffn_bs, L0_ffn_temperature, L0_ffn_query_embedding):
    import jax
    import jax.numpy as jnp

    def _L0_xattn_ref(query, key, value, Wq, bq, Wk, bk, Wv, bv, Wo, bo):
        import jax, jax.numpy as jnp
        import numpy as np
        B, S, D, H = (2, 1024, 512, 16)
        DK = D // H
        Bq, Sq, _ = query.shape
        Sk = key.shape[1]
        q = (query @ Wq + bq).reshape(Bq, Sq, H, DK)
        k = (key @ Wk + bk).reshape(Bq, Sk, H, DK)
        v = (value @ Wv + bv).reshape(Bq, Sk, H, DK)
        scores = jnp.einsum('bqhd,bkhd->hbqk', q, k) / np.sqrt(DK)
        attn = jax.nn.softmax(scores.reshape(H * Bq, Sq, Sk), axis=0).reshape(H, Bq, Sq, Sk)
        out = jnp.einsum('hbqk,bkhd->bqhd', attn, v).reshape(Bq, Sq, H * DK)
        return out @ Wo + bo

    def _L0_attn_ref(x, Wq, Wk, Wv, Eq, Ek, Ev):
        import jax, jax.numpy as jnp
        import numpy as np
        N_HEADS = 16
        MAX_DIST = 64
        B, S, D = x.shape
        H = N_HEADS
        hd = D // H
        r = jnp.arange(S)
        rel = jnp.clip(r[:, None] - r[None, :], -MAX_DIST, MAX_DIST) + MAX_DIST

        def proj(W):
            return jnp.einsum('bsd,de->bse', x, W).reshape(B, S, H, hd).transpose(0, 2, 1, 3)
        q, k, v = (proj(Wq), proj(Wk), proj(Wv))
        a_q = Eq[rel]
        a_k = Ek[rel]
        a_v = Ev[rel]
        content = jnp.einsum('bhld,bhmd->bhlm', q, k)
        rel_k = jnp.einsum('bhld,lmd->bhlm', q, a_k)
        rel_q = jnp.einsum('bhmd,lmd->bhlm', k, a_q)
        pos_pos = jnp.einsum('lmd,lmd->lm', a_q, a_k)
        scale = 1.0 / hd ** 0.5
        logits = (content + rel_k + rel_q + pos_pos) * scale
        attn = jax.nn.softmax(logits, axis=-1)
        out = jnp.einsum('bhlm,bhmd->bhld', attn, v) + jnp.einsum('bhlm,lmd->bhld', attn, a_v)
        return out.transpose(0, 2, 1, 3).reshape(B, S, D)

    def _L0_ffn_ref(x, Wq, bq, Wk, bk, Wv, bv, Wp, bp, Wr, br, Ws, bs, temperature, query_embedding):
        import jax, jax.numpy as jnp
        import numpy as np
        import math
        DIM = 512
        NUM_HEADS = 16
        SHARED_HEADS = 1
        ROUTED_HEADS = 3
        HEAD_DIM = DIM // NUM_HEADS
        B, N = (2, 1024)
        Bsz, Nn, C = x.shape
        H, hd = (NUM_HEADS, HEAD_DIM)

        def heads(W, b):
            y = x @ W.T + b
            return y.reshape(Bsz, Nn, H, hd).transpose(0, 2, 1, 3)
        q = heads(Wq, bq)
        k = heads(Wk, bk)
        v = heads(Wv, bv)
        q_norm = q / jnp.linalg.norm(q, axis=-1, keepdims=True)
        q_scaled = (q_norm + query_embedding[None]) * jax.nn.softplus(temperature)[None]
        attn = jnp.einsum('bhqd,bhkd->bhqk', q_scaled, k) / math.sqrt(hd)
        attn = jax.nn.softmax(attn, axis=-1)
        h = jnp.einsum('bhqk,bhkd->bhqd', attn, v)
        h = h.transpose(0, 2, 1, 3).reshape(Bsz, Nn, C)
        gates = jax.nn.softmax(h @ Wr.T + br, axis=-1)
        _, idx = jax.lax.top_k(gates, ROUTED_HEADS)
        mask = jax.nn.one_hot(idx, H - SHARED_HEADS, dtype=gates.dtype).sum(axis=-2)
        routed_gates = gates * mask * ROUTED_HEADS
        sw = jax.nn.softmax(h @ Ws.T + bs, axis=-1)
        shared_gates = sw * SHARED_HEADS
        weight_0 = sw * 2.0
        shared_gates = weight_0[..., 0:1] * shared_gates
        routed_gates = weight_0[..., 1:2] * routed_gates
        masked_gates = jnp.concatenate([shared_gates, routed_gates], axis=-1)
        out = h * masked_gates.sum(axis=-1, keepdims=True)
        return out @ Wp.T + bp
    x = x + _L0_xattn_ref(_layernorm(x, axis=-1), ctx_1024, ctx_1024, L0_xattn_Wq, L0_xattn_bq, L0_xattn_Wk, L0_xattn_bk, L0_xattn_Wv, L0_xattn_bv, L0_xattn_Wo, L0_xattn_bo)
    x = x + _L0_attn_ref(_layernorm(x, axis=-1), L0_attn_Wq, L0_attn_Wk, L0_attn_Wv, L0_attn_Eq, L0_attn_Ek, L0_attn_Ev)
    x = x + _L0_ffn_ref(_layernorm(x, axis=-1), L0_ffn_Wq, L0_ffn_bq, L0_ffn_Wk, L0_ffn_bk, L0_ffn_Wv, L0_ffn_bv, L0_ffn_Wp, L0_ffn_bp, L0_ffn_Wr, L0_ffn_br, L0_ffn_Ws, L0_ffn_bs, L0_ffn_temperature, L0_ffn_query_embedding)
    return x

_drawn_inputs = setup_inputs


def setup_inputs(seed=0):
    import zlib

    import numpy as np

    out = dict(_drawn_inputs(seed))
    spreads = {'L0_ffn_temperature': (4.151041507720947, 0.6)}
    factors = {'L0_xattn_bo': 24.718,
     'L0_attn_Wq': 8.0,
     'L0_attn_Wk': 8.0,
     'L0_attn_Wv': 2.979,
     'L0_attn_Eq': 64.0,
     'L0_attn_Ek': 64.0,
     'L0_attn_Ev': 64.0,
     'L0_ffn_Wq': 138.682,
     'L0_ffn_bq': 200.0,
     'L0_ffn_Wk': 26.143,
     'L0_ffn_bk': 200.0,
     'L0_ffn_bv': 28.361,
     'L0_ffn_bp': 45.671,
     'L0_ffn_Wr': 200.0,
     'L0_ffn_br': 200.0,
     'L0_ffn_Ws': 8.0,
     'L0_ffn_bs': 200.0,
     'L0_ffn_query_embedding': 89.801}
    for name, (base, spread) in spreads.items():
        noise = np.random.default_rng([zlib.crc32(name.encode()), seed]).standard_normal(out[name].shape)
        drawn = base * np.exp(spread * noise) if base else spread * noise
        out[name] = jnp.asarray(drawn.astype(out[name].dtype))
    for name, factor in factors.items():
        out[name] = (out[name] * factor).astype(out[name].dtype)
    return out
```

```python
from contextlib import ExitStack

import concourse.bass as bass
import numpy as np
from concourse import mybir

F32 = mybir.dt.float32
ACT = mybir.ActivationFunctionType
ALU = mybir.AluOpType
AX = mybir.AxisListType

P = 128
B = 4
D = 512
C = D // P
H = 16
HD = D // H
J = P // HD
G = B * C
SK = 2048
T = SK // P
NR = 15
NG = NR + 2
EPS = 1e-5
SCALE = float(HD) ** -0.5


def program(nc, a, out):
    with ExitStack() as ctx:
        def sb(name, shape, dt=F32):
            return ctx.enter_context(nc.sbuf_tensor(name, shape, dt))

        def sem(name):
            return ctx.enter_context(nc.semaphore(name))

        x_res = sb("x_res", [P, B, D])
        q_blocks = sb("q_blocks", [P, G, J, P])
        probs_t = q_blocks
        s_buf = sb("s_buf", [P, 2, B * H, P])
        ctx_kt = sb("ctx_kt", [P, 4, C, D])
        ctx_t = ctx_kt[:, 0:2]
        k_t = ctx_kt[:, 2:4]
        k_blocks = ctx_kt[:, :, :, :].rearrange("p a c (j l) -> p (a c) j l", j=J)
        v_buf = sb("v_buf", [P, 2, B, D])
        w_q, w_k, w_v, w_o = (sb(f"w_{n}", [P, C, D]) for n in "qkvo")
        extra = sb("extra", [P, 4096])
        pool_tmp = extra[:, 0:2048]
        bv_all = extra[:, 2048:2560]
        bo_all = extra[:, 2560:3072]
        m_part = extra[:, 3072:3584].rearrange("p (b q) -> p b q", b=B)
        z_part = extra[:, 3584:3968].rearrange("p (n q) -> p n q", n=3)
        ev_rel = extra[:, :].rearrange("p (l d) -> p l d", d=HD)
        bias3 = extra[:, 0:2048].rearrange("p (n e) -> p n e", n=4)
        ident = sb("ident", [P, P])
        m_all = sb("m_all", [P, P])
        r_all = sb("r_all", [P, P])
        ek_tab = sb("ek_tab", [P, 2 * P - 1])
        eq_tab = sb("eq_tab", [P, 2 * P - 1])
        pos = sb("pos", [P, P])
        cols = sb("cols", [P, 3, C])
        stats = sb("stats", [P, B, 6])
        mean_var = sb("mean_var", [P, B, 2])
        rstd = sb("rstd", [P, B])
        temp = sb("temp", [P, H])
        soft = sb("soft", [P, 3, H])
        rmax = sb("rmax", [P, B * H])
        rsum = sb("rsum", [P, B * H])
        rinv = sb("rinv", [P, B * H])
        w_gate = sb("w_gate", [P, C, NG])
        b_gate = sb("b_gate", [P, NG])
        gate = sb("gate", [P, B, NG])
        gtmp = sb("gtmp", [P, B, 8])
        top8 = sb("top8", [P, B, 8])
        ps = ctx.enter_context(nc.psum_tensor("ps", [P, 8, 512], F32))

        y_ln = v_buf[:, 1]
        x_t0 = s_buf[:, 0, 0:16, :].rearrange("p (c b) q -> p c (b q)", c=C)
        x_t = v_buf[:, 0].rearrange("p b (c q) -> p b c q", c=C).rearrange("p b c q -> p (b c q)").rearrange(
            "p (c n) -> p c n", c=C)
        eq_rel = s_buf[:, 1, 0:32, :].rearrange("p h (m d) -> p (h m) d", d=HD)
        ek_rel = s_buf[:, 1, 32:64, :].rearrange("p h (m d) -> p (h m) d", d=HD)

        ctx_ready = [sem("ctx_ready0"), sem("ctx_ready1")]
        names = """x_in wq_in wk_in wv_in wo_in cols_in bv_in bo_in tab_in rel_in small_in
            ident_done qzero kzero stats_done mv_done var_done std_done rstd_done ln_done tr_done tr_evac q_psum q_evac xb_done
            pos_mul pos_done
            kv_psum kv_evac v_ready s_psum s_evac max_done m_ready sub_done exp_done
            sum_dve zadd zmore zpool z_done r_ready attn_dve attn_pool av_done
            ot_evac wo_psum x1_done
            wq2_in wk2_in wv2_in ev_in
            q2_psum q2_evac q2_blocks k2_psum k2_blocks v2_psum v2_evac
            rk_psum rk_evac rq_psum rq_evac lg_psum lg_done max2 sub2_dve sub2_pool exp2 sum2 rinv2
            at_psum at_act at_dve av2 ev2 ot2_evac ot2_done back_psum back_mul x2_done
            soft_a soft_b soft_c soft_d soft_e
            wq3_in wk3_in wv3_in wp3_in b3_in xp_done
            q3_psum q3_bias q3_sq q3_ss q3_rt q3_rn q3_a q3_b q3_done q3t_psum q3t_evac k3_psum k3_blocks v3_psum v3_done
            lg3_psum max3 sub3 exp3 sum3 rinv3 nrm3_dve nrm3_pool at3_psum at3_act at3_dve av3 ot3_evac
            g_psum g_bias g_max g_sub g_exp g_top g_c1 g_c2 g_c3 g_c4 g_c5 g_c6 y_psum fin_done out_done""".split()
        s = {n: sem(n) for n in names}

        block = ctx.enter_context(nc.Block())

        def at_row(blocks, row):
            return blocks[:, :, :, row].rearrange("p g j -> p (g j)")

        def schedule(eng, first, stage, last):
            first()
            stage(0, 0)
            with eng.Fori(0, (T - 2) // 2) as i:
                stage(2 * i + 1, 1)
                stage(2 * i + 2, 0)
            last()

        @block.sync
        def _(sp):
            def load(dst, src, name):
                sp.dma_start(dst, src).then_inc(s[name], 16)

            load(x_res[:], a["x"].rearrange("b q e -> q b e"), "x_in")
            load(cols[:], a["cols"], "cols_in")
            load(w_q[:], a["Wq1"], "wq_in")
            load(w_k[:], a["Wk1"], "wk_in")
            sp.dma_start(ctx_t[:, 0], a["ctxT"][0]).then_inc(ctx_ready[0], 16)
            load(w_v[:], a["Wv1"], "wv_in")
            load(bv_all, a["bv1"].partition_broadcast(P), "bv_in")
            sp.dma_start(ctx_t[:, 1], a["ctxT"][1]).then_inc(ctx_ready[1], 16)
            load(bo_all, a["bo1"].partition_broadcast(P), "bo_in")
            load(w_o[:], a["Wo1"], "wo_in")
            load(eq_rel, a["EqRel"], "rel_in")
            load(ek_rel, a["EkRel"], "rel_in")
            load(eq_tab[:], a["EqTab"], "tab_in")
            load(ek_tab[:], a["EkTab"], "tab_in")
            load(temp[:], a["temp"].partition_broadcast(P), "small_in")
            load(w_gate[:], a["Wg"], "small_in")
            load(b_gate[:], a["bg"].partition_broadcast(P), "small_in")
            def ctx_load(t, p):
                sp.wait_ge(s["kv_psum"], 8 * t + 8)
                sp.dma_start(ctx_t[:, p], a["ctxT"][t + 2]).then_inc(ctx_ready[p], 16)

            with sp.Fori(0, (T - 2) // 2) as i:
                ctx_load(2 * i, 0)
                ctx_load(2 * i + 1, 1)
            sp.wait_ge(s["q_psum"], C)
            load(w_q[:], a["Wq2"], "wq2_in")
            sp.wait_ge(s["kv_psum"], 8 * T)
            load(w_k[:], a["Wk2"], "wk2_in")
            load(w_v[:], a["Wv2"], "wv2_in")
            sp.wait_ge(s["attn_pool"], T)
            sp.wait_ge(s["zpool"], T)
            sp.wait_ge(s["v_ready"], B * T)
            sp.wait_ge(s["xb_done"], 1)
            load(ev_rel, a["EvRel"], "ev_in")
            sp.wait_ge(s["q2_psum"], C)
            load(w_q[:], a["Wq3"], "wq3_in")
            sp.wait_ge(s["k2_psum"], C)
            load(w_k[:], a["Wk3"], "wk3_in")
            sp.wait_ge(s["v2_psum"], B)
            load(w_v[:], a["Wv3"], "wv3_in")
            sp.wait_ge(s["lg_psum"], G)
            load(w_o[:], a["Wp3"], "wp3_in")
            sp.wait_ge(s["ev2"], 4)
            load(bias3, a["bias3"].rearrange("(o n) e -> o n e", o=1).broadcast_to([P, 4, D]), "b3_in")
            for b in range(B):
                sp.wait_ge(s["fin_done"], b + 1)
                sp.dma_start(out[b], x_res[:, b, :]).then_inc(s["out_done"], 16)
            sp.wait_ge(s["out_done"], 16 * B)

        @block.tensor
        def _(pe):
            mm = nc.tensor.matmul

            def ln_transposes(k, dst_banks):
                for c in range(C):
                    for b in range(B):
                        if c == 0:
                            pe.wait_ge(s["ln_done"], B * k + b + 1)
                        last = nc.tensor.transpose(ps[:, dst_banks + c, b * P:(b + 1) * P],
                                                   y_ln[:, b, c * P:(c + 1) * P], ident[:])
                    last.then_inc(s["tr_done"], 1)

            def proj_t(w, src, bank, done, hg):
                for c in range(C):
                    last = mm(ps[:, bank, :], w[:, c, hg * P:(hg + 1) * P], src[:, c, :], start=c == 0, stop=c == C - 1)
                last.then_inc(done, 1)

            def proj_n(w, src, bank, done, b):
                for c in range(C):
                    last = mm(ps[:, bank, :], src[:, c, b * P:(b + 1) * P], w[:, c, :], start=c == 0, stop=c == C - 1)
                last.then_inc(done, 1)

            pe.wait_ge(s["ident_done"], 2)
            ln_transposes(0, 4)
            pe.wait_ge(s["wq_in"], 16)
            for hg in range(C):
                pe.wait_ge(s["tr_evac"], C)
                proj_t(w_q, x_t0, hg, s["q_psum"], hg)

            def project(t, p, pair):
                pe.wait_ge(ctx_ready[p], 16 * pair + 16)
                for n in range(8):
                    if n < 2:
                        if isinstance(t, int) and t == 0:
                            pe.wait_ge(s["q_evac"], 4 * (n + 1))
                        else:
                            pe.wait_ge(s["kv_evac"], 8 * t + n - 1)
                    else:
                        pe.wait_ge(s["kv_evac"], 8 * t + n - 1)
                    if n < 4:
                        proj_t(w_k, ctx_t[:, p], n % 2, s["kv_psum"], n)
                    else:
                        b = n - 4
                        for c in range(C):
                            last = mm(ps[:, n % 2, :], ctx_t[:, p, c, b * P:(b + 1) * P], w_v[:, c, :],
                                      start=c == 0, stop=c == C - 1)
                        last.then_inc(s["kv_psum"], 1)

            def score(t, p):
                for g in range(G):
                    b, hg = divmod(g, C)
                    if b == 0:
                        pe.wait_ge(s["kv_evac"], 8 * t + hg + 1)
                    if g >= 2:
                        pe.wait_ge(s["s_evac"], 16 * t + g - 1)
                    elif not (isinstance(t, int) and t == 0):
                        pe.wait_ge(s["s_evac"], 16 * t + g - 1)
                    mm(ps[:, 2 + g % 2, :], k_t[:, p, hg, b * P:(b + 1) * P],
                       q_blocks[:, g].rearrange("p j q -> p (j q)"), start=True, stop=True).then_inc(s["s_psum"], 1)

            def attend(t, p, first=False, final=False):
                for b in range(B):
                    pe.wait_ge(s["v_ready"], B * t + b + 1)
                    if b < 3:
                        pe.wait_ge(s["attn_dve"], 3 * t + b + 1)
                    else:
                        pe.wait_ge(s["attn_pool"], t + 1)
                    for hg in range(C):
                        for j in range(J):
                            h = hg * J + j
                            last = mm(ps[j * HD:(j + 1) * HD, 4 + b, hg * P:(hg + 1) * P],
                                      v_buf[:, p, b, h * HD:(h + 1) * HD], s_buf[:, p, b * H + h, :],
                                      start=first and hg == 0, stop=final and hg == C - 1, skip_group_check=True)
                    last.then_inc(s["av_done"], 1)

            def first():
                pe.wait_ge(s["wk_in"], 16)
                pe.wait_ge(s["wv_in"], 16)
                pe.wait_ge(s["q_evac"], 16)
                project(0, 0, 0)
                score(0, 0)

            def stage(t, p, pair):
                project(t + 1, 1 - p, pair)
                score(t + 1, 1 - p)
                attend(t, p, first=isinstance(t, int) and t == 0)

            first()
            stage(0, 0, 0)
            with pe.Fori(0, (T - 2) // 2) as i:
                stage(2 * i + 1, 1, i + 1)
                stage(2 * i + 2, 0, i + 1)
            attend(T - 1, 1, final=True)

            pe.wait_ge(s["wo_in"], 16)
            for b in range(B):
                pe.wait_ge(s["ot_evac"], b + 1)
                for hg in range(C):
                    last = mm(ps[:, b, :], s_buf[:, 0, b * C + hg, :], w_o[:, hg, :], start=hg == 0, stop=hg == C - 1)
                last.then_inc(s["wo_psum"], 1)

            ln_transposes(1, 4)
            for hg in range(C):
                pe.wait_ge(s["tr_evac"], 2 * C)
                pe.wait_ge(s["x1_done"], hg + 1)
                if hg == 0:
                    pe.wait_ge(s["wq2_in"], 16)
                proj_t(w_q, x_t, hg, s["q2_psum"], hg)
            pe.wait_ge(s["wk2_in"], 16)
            for hg in range(C):
                proj_t(w_k, x_t, 4 + hg, s["k2_psum"], hg)
            pe.wait_ge(s["wv2_in"], 16)
            for b in range(B):
                pe.wait_ge(s["q2_evac"], b + 1)
                proj_n(w_v, x_t, b, s["v2_psum"], b)
            pe.wait_ge(s["tab_in"], 32)
            pe.wait_ge(s["q2_blocks"], 16)

            def relative(table, blocks, psum_done, drained):
                for n in range(P // 4):
                    drained(n)
                    for i in range(4):
                        r = 4 * n + i
                        rows = at_row(blocks, r).rearrange("p (o n) -> p o n", o=1).broadcast_to([P, 2, B * H])
                        last = mm(ps[:, n % 8, i * P:(i + 1) * P].rearrange("p (o n) -> p o n", o=2),
                                  table[:, P - 1 - r:2 * P - 1 - r], rows, start=True, stop=True)
                    last.then_inc(psum_done, 1)

            def rk_free(n):
                if n < 4:
                    pe.wait_ge(s["v2_evac"], n + 1)
                elif n < 8:
                    pe.wait_ge(s["k2_blocks"], 4 * (n - 4) + 4)
                else:
                    pe.wait_ge(s["rk_evac"], n - 7)

            def rq_free(n):
                if n < 8:
                    pe.wait_ge(s["rk_evac"], 24 + n + 1)
                else:
                    pe.wait_ge(s["rq_evac"], n - 7)

            relative(ek_tab, q_blocks, s["rk_psum"], rk_free)
            pe.wait_ge(s["k2_blocks"], 16)
            relative(eq_tab, k_blocks, s["rq_psum"], rq_free)
            for g in range(G):
                b, hg = divmod(g, C)
                if g < 8:
                    pe.wait_ge(s["rq_evac"], 24 + g + 1)
                else:
                    pe.wait_ge(s["lg_done"], g - 7)
                mm(ps[:, g % 8, :], w_o[:, hg, b * P:(b + 1) * P], k_blocks[:, g].rearrange("p j m -> p (j m)"),
                   start=True, stop=False, skip_group_check=True)
                for j in range(J):
                    last = mm(ps[:, g % 8, j * P:(j + 1) * P], s_buf[:, 1, g * J + j, :], ident[:],
                              start=False, stop=j == J - 1, skip_group_check=True)
                last.then_inc(s["lg_psum"], 1)
            for g in range(G):
                if g < 4:
                    pe.wait_ge(s["lg_done"], G)
                else:
                    pe.wait_ge(s["at_act"], (g - 4) // 2 + 1) if g % 2 == 0 else pe.wait_ge(s["at_dve"], (g - 4) // 2 + 1)
                pe.wait_ge(s["exp2"], g // C + 1)
                for j in range(J):
                    last = nc.tensor.transpose(ps[:, g % 4, j * P:(j + 1) * P], s_buf[:, 0, g * J + j, :], ident[:])
                last.then_inc(s["at_psum"], 1)
            for g in range(G):
                b, hg = divmod(g, C)
                if g % 2 == 0:
                    pe.wait_ge(s["at_act"], g // 2 + 1)
                else:
                    pe.wait_ge(s["at_dve"], g // 2 + 1)
                for j in range(J):
                    h = hg * J + j
                    last = mm(ps[j * HD:(j + 1) * HD, 4 + b, hg * P:(hg + 1) * P], v_buf[:, 1, b, h * HD:(h + 1) * HD],
                              probs_t[:, g, j, :], start=hg == 0, stop=hg == C - 1, skip_group_check=True)
                if hg == C - 1:
                    last.then_inc(s["av2"], 1)
            pe.wait_ge(s["ev_in"], 16)
            for bank in range(4):
                for n in range(32):
                    l, i = bank * 32 + n, n % 4
                    last = mm(ps[i * HD:(i + 1) * HD, bank, n // 4 * 64:(n // 4 + 1) * 64], ev_rel[:, l, :],
                              at_row(probs_t, l), start=n < 4, stop=n >= 28, skip_group_check=True)
                last.then_inc(s["ev2"], 1)
            for b in range(B):
                pe.wait_ge(s["ot2_done"], 16)
                for hg in range(C):
                    last = nc.tensor.transpose(ps[:, 4 + b, hg * P:(hg + 1) * P], s_buf[:, 1, b * C + hg, :], ident[:])
                last.then_inc(s["back_psum"], 1)

            for c in range(C):
                for b in range(B):
                    if c == 0:
                        pe.wait_ge(s["ln_done"], 2 * B + b + 1)
                    last = nc.tensor.transpose(ps[:, c, b * P:(b + 1) * P], y_ln[:, b, c * P:(c + 1) * P], ident[:])
                last.then_inc(s["tr_done"], 1)
            pe.wait_ge(s["tr_evac"], 3 * C)
            pe.wait_ge(s["wq3_in"], 16)
            for b in range(B):
                pe.wait_ge(s["back_mul"], b + 1)
                proj_n(w_q, x_t, 4 + b, s["q3_psum"], b)
            pe.wait_ge(s["wk3_in"], 16)
            for hg in range(C):
                proj_t(w_k, x_t, hg, s["k3_psum"], hg)
            pe.wait_ge(s["wv3_in"], 16)
            for b in range(B):
                pe.wait_ge(s["q3_bias"], b + 1)
                proj_n(w_v, x_t, 4 + b, s["v3_psum"], b)
            for c in range(C):
                pe.wait_ge(s["k3_blocks"], 4 * c + 4)
                for b in range(B):
                    pe.wait_ge(s["q3_done"], 1)
                    last = nc.tensor.transpose(ps[:, c, b * P:(b + 1) * P], s_buf[:, 1, b * C + c, :], ident[:])
                last.then_inc(s["q3t_psum"], 1)
            pe.wait_ge(s["q3t_evac"], C)
            for g in range(G):
                b, hg = divmod(g, C)
                if b == 1:
                    pe.wait_ge(s["v3_done"], B)
                if b >= 2:
                    pe.wait_ge(s["sub3"], b - 1)
                mm(ps[:, 4 * (b % 2) + hg, :], s_buf[:, 1, 32 + 4 * hg + b, :],
                   k_blocks[:, g].rearrange("p j m -> p (j m)"), start=True, stop=True).then_inc(s["lg3_psum"], 1)
            for g in range(G):
                if g < 4:
                    pe.wait_ge(s["sub3"], B)
                else:
                    pe.wait_ge(s["at3_act"] if g % 2 == 0 else s["at3_dve"], (g - 4) // 2 + 1)
                if g // C < 2:
                    pe.wait_ge(s["nrm3_dve"], g // C + 1)
                else:
                    pe.wait_ge(s["nrm3_pool"], g // C - 1)
                for j in range(J):
                    last = nc.tensor.transpose(ps[:, g % 4, j * P:(j + 1) * P], s_buf[:, 0, g * J + j, :], ident[:])
                last.then_inc(s["at3_psum"], 1)
            for g in range(G):
                b, hg = divmod(g, C)
                pe.wait_ge(s["at3_act"] if g % 2 == 0 else s["at3_dve"], g // 2 + 1)
                for j in range(J):
                    h = hg * J + j
                    last = mm(ps[j * HD:(j + 1) * HD, 4 + b, hg * P:(hg + 1) * P], v_buf[:, 1, b, h * HD:(h + 1) * HD],
                              probs_t[:, g, j, :], start=hg == 0, stop=hg == C - 1, skip_group_check=True)
                if hg == C - 1:
                    last.then_inc(s["av3"], 1)
            pe.wait_ge(s["small_in"], 48)
            for b in range(B):
                pe.wait_ge(s["ot3_evac"], b + 1)
                for hg in range(C):
                    last = mm(ps[:, 4 + b, 0:NG], s_buf[:, 1, b * C + hg, :], w_gate[:, hg, :],
                              start=hg == 0, stop=hg == C - 1)
                last.then_inc(s["g_psum"], 1)
            pe.wait_ge(s["wp3_in"], 16)
            for b in range(B):
                for hg in range(C):
                    last = mm(ps[:, b, :], s_buf[:, 1, b * C + hg, :], w_o[:, hg, :], start=hg == 0, stop=hg == C - 1)
                last.then_inc(s["y_psum"], 1)

        @block.scalar
        def _(act):
            copy = nc.scalar.copy

            def ln_std(k):
                act.wait_ge(s["var_done"], k + 1)
                nc.scalar.activation(rstd[:], rstd[:], ACT.Sqrt).then_inc(s["std_done"], 1)

            ln_std(0)
            for c in range(C):
                act.wait_ge(s["tr_done"], c + 1)
                copy(x_t0[:, c, :], ps[:, 4 + c, :]).then_inc(s["tr_evac"], 1)

            def kv_copy(t, p, n):
                act.wait_ge(s["kv_psum"], 8 * t + n + 1)
                if n < 4:
                    if not (isinstance(t, int) and t <= 1):
                        act.wait_ge(s["s_psum"], 16 * (t - 1))
                    nc.scalar.activation(k_t[:, p, n, :], ps[:, n % 2, :], ACT.Identity,
                                         bias=cols[:, 1, n:n + 1]).then_inc(s["kv_evac"], 1)
                else:
                    if not (isinstance(t, int) and t <= 1):
                        act.wait_ge(s["av_done"], 4 * (t - 1))
                    copy(v_buf[:, p, n - 4, :], ps[:, n % 2, :]).then_inc(s["kv_evac"], 1)

            def s_copy(t, p):
                for g in range(G):
                    if g % C == 0 and not (isinstance(t, int) and t <= 1):
                        act.wait_ge(s["av_done"], 4 * (t - 2) + g // C + 1)
                    act.wait_ge(s["s_psum"], 16 * t + g + 1)
                    copy(s_buf[:, p, g * J:(g + 1) * J, :], ps[:, 2 + g % 2, :]).then_inc(s["s_evac"], 1)

            def exp(t, p, b):
                act.wait_ge(s["sub_done"], 4 * t + b + 1)
                part = s_buf[:, p, b * H:(b + 1) * H, :]
                nc.scalar.activation(part, part, ACT.Exp).then_inc(s["exp_done"], 1)

            def first():
                act.wait_ge(s["cols_in"], 16)
                act.wait_ge(s["ln_done"], B)
                for n in range(8):
                    kv_copy(0, 0, n)
                act.wait_ge(s["q_psum"], C)
                s_copy(0, 0)

            def stage(t, p):
                for n in range(8):
                    kv_copy(t + 1, 1 - p, n)
                    if n in (1, 2, 3, 4):
                        exp(t, p, n - 1)
                if isinstance(t, int):
                    act.wait_ge(s["pos_done"], 1)
                s_copy(t + 1, 1 - p)

            def last():
                for b in range(B):
                    exp(T - 1, 1, b)

            schedule(act, first, stage, last)

            for b in range(B):
                act.wait_ge(s["av_done"], B * (T - 1) + b + 1)
                copy(s_buf[:, 0, b * C:(b + 1) * C, :], ps[:, 4 + b, :]).then_inc(s["ot_evac"], 1)
            act.wait_ge(s["soft_a"], 1)
            nc.scalar.activation(soft[:, 1], soft[:, 0], ACT.Exp).then_inc(s["soft_b"], 1)
            act.wait_ge(s["soft_b"], 1)
            nc.scalar.activation(soft[:, 2], soft[:, 1], ACT.Ln, bias=1.0).then_inc(s["soft_c"], 1)

            ln_std(1)
            for c in range(C):
                act.wait_ge(s["tr_done"], C + c + 1)
                copy(x_t[:, c, :], ps[:, 4 + c, :]).then_inc(s["tr_evac"], 1)
            act.wait_ge(s["wo_psum"], B)
            for hg in range(C):
                act.wait_ge(s["q2_psum"], hg + 1)
                copy(w_o[:, hg, :], ps[:, hg, :]).then_inc(s["q2_evac"], 1)
            for b in range(B):
                act.wait_ge(s["v2_psum"], b + 1)
                copy(v_buf[:, 1, b, :], ps[:, b, :]).then_inc(s["v2_evac"], 1)
            for n in range(P // 4):
                act.wait_ge(s["rk_psum"], n + 1)
                copy(s_buf[:, 1, :, 4 * n:4 * n + 4].rearrange("p n l -> p l n"),
                     ps[:, n % 8, :].rearrange("p (l o n) -> p l o n", l=4, o=2)[:, :, 0, :]).then_inc(s["rk_evac"], 1)
            for b in range(B):
                act.wait_ge(s["sub2_dve"] if b < 2 else s["sub2_pool"], b % 2 + 1)
                part = s_buf[:, 0, b * H:(b + 1) * H, :]
                nc.scalar.activation(part, part, ACT.Exp, scale=SCALE).then_inc(s["exp2"], 1)
            for g in range(0, G, 2):
                act.wait_ge(s["at_psum"], g + 1)
                copy(probs_t[:, g, :, :], ps[:, g % 4, :]).then_inc(s["at_act"], 1)
            for b in range(B):
                act.wait_ge(s["av2"], b + 1)
                copy(s_buf[:, 1, b * C:(b + 1) * C, :], ps[:, 4 + b, :]).then_inc(s["ot2_evac"], 1)

            ln_std(2)
            for c in range(C):
                act.wait_ge(s["tr_done"], 2 * C + c + 1)
                copy(x_t[:, c, :], ps[:, c, :]).then_inc(s["tr_evac"], 1)
            act.wait_ge(s["q3_bias"], B)
            nc.scalar.activation(s_buf[:, 1, 16:32, :], s_buf[:, 1, 0:16, :], ACT.Square).then_inc(s["q3_sq"], 1)
            act.wait_ge(s["q3_ss"], 1)
            nc.scalar.activation(rsum[:], rsum[:], ACT.Sqrt).then_inc(s["q3_rt"], 1)
            for c in range(C):
                act.wait_ge(s["q3t_psum"], c + 1)
                copy(s_buf[:, 1, 32 + 4 * c:36 + 4 * c, :], ps[:, c, :]).then_inc(s["q3t_evac"], 1)
            for b in range(B):
                act.wait_ge(s["sub3"], b + 1)
                part = s_buf[:, 0, b * H:(b + 1) * H, :]
                nc.scalar.activation(part, part, ACT.Exp, scale=SCALE).then_inc(s["exp3"], 1)
            for g in range(0, G, 2):
                act.wait_ge(s["at3_psum"], g + 1)
                copy(probs_t[:, g, :, :], ps[:, g % 4, :]).then_inc(s["at3_act"], 1)
            for b in range(B):
                act.wait_ge(s["av3"], b + 1)
                copy(s_buf[:, 1, b * C:(b + 1) * C, :], ps[:, 4 + b, :]).then_inc(s["ot3_evac"], 1)
            act.wait_ge(s["g_sub"], 2)
            nc.scalar.activation(gate[:], gate[:], ACT.Exp).then_inc(s["g_exp"], 1)

        @block.gpsimd
        def _(pool):
            pool.memset(ident[:], 0.0).then_inc(s["ident_done"], 1)
            pool.wait_ge(s["ident_done"], 1)
            pool.affine_select(out=ident[:], in_=ident[:], compare_op=ALU.not_equal, fill=1.0, base=0,
                               pattern=[[-1, P]], channel_multiplier=1).then_inc(s["ident_done"], 1)

            pool.memset(q_blocks[:], 0.0).then_inc(s["qzero"], 1)
            pool.wait_ge(s["ln_done"], B)
            pool.wait_ge(s["bo_in"], 16)
            bo = bo_all.rearrange("p (o e) -> p o e", o=1).broadcast_to([P, B, D])
            pool.tensor_tensor(x_res[:], x_res[:], bo, ALU.add).then_inc(s["xb_done"], 1)
            pool.wait_ge(s["bv_in"], 16)

            def v_bias(t, p):
                for b in range(B):
                    pool.wait_ge(s["kv_evac"], 8 * t + 4 + b + 1)
                    pool.tensor_tensor(v_buf[:, p, b, :], v_buf[:, p, b, :], bv_all, ALU.add).then_inc(s["v_ready"], 1)

            def sum_half(t, p):
                pool.wait_ge(s["exp_done"], 4 * t + 4)
                acc = pool_tmp.rearrange("p (h q) -> p h q", q=P)
                pool.tensor_tensor(acc, s_buf[:, p, 2 * H:3 * H, :], s_buf[:, p, 3 * H:4 * H, :],
                                   ALU.add).then_inc(s["zadd"], 1)
                for n, w in enumerate((8, 4, 2)):
                    pool.wait_ge(s["zadd"], 4 * t + n + 1)
                    pool.tensor_tensor(acc[:, 0:w], acc[:, 0:w], acc[:, w:2 * w], ALU.add).then_inc(s["zadd"], 1)
                pool.wait_ge(s["zadd"], 4 * t + 4)
                if not (isinstance(t, int) and t == 0):
                    pool.wait_ge(s["z_done"], 2 * t)
                pool.tensor_tensor(z_part[:, 2], acc[:, 0], acc[:, 1], ALU.add).then_inc(s["zpool"], 1)

            def normalise(t, p):
                pool.wait_ge(s["r_ready"], t + 1)
                part = s_buf[:, p, 3 * H:4 * H, :]
                r = r_all[:, :].rearrange("p (o q) -> p o q", o=1).broadcast_to([P, H, P])
                pool.tensor_tensor(part, part, r, ALU.mult).then_inc(s["attn_pool"], 1)

            def first():
                v_bias(0, 0)

            def stage(t, p):
                sum_half(t, p)
                normalise(t, p)
                v_bias(t + 1, 1 - p)

            def last():
                pool.wait_ge(s["s_psum"], 16 * T)
                pool.wait_ge(s["kv_psum"], 8 * T)
                pool.memset(k_blocks, 0.0).then_inc(s["kzero"], 1)
                sum_half(T - 1, 1)
                normalise(T - 1, 1)

            schedule(pool, first, stage, last)

            for b in (2, 3):
                pool.wait_ge(s["max2"], b + 1)
                part = s_buf[:, 0, b * H:(b + 1) * H, :]
                m = rmax[:, b * H:(b + 1) * H].rearrange("p (h o) -> p h o", o=1).broadcast_to([P, H, P])
                pool.tensor_tensor(part, part, m, ALU.subtract).then_inc(s["sub2_pool"], 1)
            pool.wait_ge(s["ln_done"], 3 * B)
            pool.wait_ge(s["b3_in"], 16)
            bp = bias3[:, 3:4, :].broadcast_to([P, B, D])
            pool.tensor_tensor(x_res[:], x_res[:], bp, ALU.add).then_inc(s["xp_done"], 1)
            for b in (2, 3):
                pool.wait_ge(s["rinv3"], b + 1)
                part = s_buf[:, 0, b * H:(b + 1) * H, :]
                r = rinv[:, b * H:(b + 1) * H].rearrange("p (h o) -> p h o", o=1).broadcast_to([P, H, P])
                pool.tensor_tensor(part, part, r, ALU.mult).then_inc(s["nrm3_pool"], 1)

        @block.vector
        def _(dve):
            tt = nc.vector.tensor_tensor

            def layer_norm(k, ready):
                for b in range(B):
                    ready(b)
                    nc.vector.bn_stats(stats[:, b, :], x_res[:, b, :]).then_inc(s["stats_done"], 1)
                for b in range(B):
                    dve.wait_ge(s["stats_done"], B * k + b + 1)
                    nc.vector.bn_aggr(mean_var[:, b, :], stats[:, b, :]).then_inc(s["mv_done"], 1)
                dve.wait_ge(s["mv_done"], B * (k + 1))
                nc.vector.tensor_scalar(rstd[:], mean_var[:, :, 1], EPS, None, ALU.add).then_inc(s["var_done"], 1)
                dve.wait_ge(s["std_done"], k + 1)
                nc.vector.reciprocal(rstd[:], rstd[:]).then_inc(s["rstd_done"], 1)
                dve.wait_ge(s["rstd_done"], k + 1)
                for b in range(B):
                    nc.vector.tensor_scalar(y_ln[:, b, :], x_res[:, b, :], mean_var[:, b, 0:1], rstd[:, b:b + 1],
                                            ALU.subtract, ALU.mult).then_inc(s["ln_done"], 1)

            dve.wait_ge(s["x_in"], 16)
            layer_norm(0, lambda b: None)
            dve.wait_ge(s["qzero"], 1)
            dve.wait_ge(s["cols_in"], 16)
            for hg in range(C):
                dve.wait_ge(s["q_psum"], hg + 1)
                for j in range(J):
                    rows = slice(j * HD, (j + 1) * HD)
                    nc.vector.tensor_scalar(q_blocks[rows, hg::C, j, :],
                                            ps[rows, hg, :].rearrange("p (b q) -> p b q", b=B),
                                            cols[rows, 0, hg:hg + 1], SCALE, ALU.add, ALU.mult).then_inc(s["q_evac"], 1)
            dve.wait_ge(s["rel_in"], 32)
            tt(eq_rel, eq_rel, ek_rel, ALU.mult).then_inc(s["pos_mul"], 1)
            dve.wait_ge(s["pos_mul"], 1)
            nc.vector.tensor_reduce(pos[:], eq_rel, AX.X, ALU.add).then_inc(s["pos_done"], 1)
            dve.wait_ge(s["small_in"], 48)
            nc.vector.scalar_tensor_tensor(soft[:, 0], temp[:], -1.0, temp[:], ALU.mult, ALU.min).then_inc(s["soft_a"], 1)

            def over_heads(t):
                return t[:, :].rearrange("p (o q) -> p o q", o=1).broadcast_to([P, H, P])

            def maxima(t, p):
                for b in range(B):
                    dve.wait_ge(s["s_evac"], 16 * t + 4 * b + 4)
                    nc.vector.tensor_reduce(m_part[:, b, :], s_buf[:, p, b * H:(b + 1) * H, :].rearrange("p h q -> p q h"),
                                            AX.X, ALU.max).then_inc(s["max_done"], 1)
                dve.wait_ge(s["max_done"], 4 * t + 4)
                nc.vector.tensor_reduce(m_all[:], m_part[:, :, :].rearrange("p b q -> p q b"), AX.X,
                                        ALU.max).then_inc(s["m_ready"], 1)

            def softmax(t, p):
                dve.wait_ge(s["m_ready"], t + 1)
                for b in range(B):
                    part = s_buf[:, p, b * H:(b + 1) * H, :]
                    tt(part, part, over_heads(m_all), ALU.subtract).then_inc(s["sub_done"], 1)
                for b in range(2):
                    dve.wait_ge(s["exp_done"], 4 * t + b + 1)
                    nc.vector.tensor_reduce(z_part[:, b, :], s_buf[:, p, b * H:(b + 1) * H, :].rearrange("p h q -> p q h"),
                                            AX.X, ALU.add).then_inc(s["sum_dve"], 1)
                dve.wait_ge(s["sum_dve"], 2 * t + 2)
                tt(z_part[:, 0], z_part[:, 0], z_part[:, 1], ALU.add).then_inc(s["z_done"], 1)
                dve.wait_ge(s["z_done"], 2 * t + 1)
                dve.wait_ge(s["zpool"], t + 1)
                tt(z_part[:, 0], z_part[:, 0], z_part[:, 2], ALU.add).then_inc(s["z_done"], 1)
                dve.wait_ge(s["z_done"], 2 * t + 2)
                if not (isinstance(t, int) and t == 0):
                    dve.wait_ge(s["attn_pool"], t)
                nc.vector.reciprocal(r_all[:], z_part[:, 0]).then_inc(s["r_ready"], 1)
                dve.wait_ge(s["r_ready"], t + 1)
                for b in range(3):
                    part = s_buf[:, p, b * H:(b + 1) * H, :]
                    tt(part, part, over_heads(r_all), ALU.mult).then_inc(s["attn_dve"], 1)

            def first():
                maxima(0, 0)

            def stage(t, p):
                softmax(t, p)
                maxima(t + 1, 1 - p)

            def last():
                softmax(T - 1, 1)

            schedule(dve, first, stage, last)

            dve.wait_ge(s["xb_done"], 1)
            for b in range(B):
                dve.wait_ge(s["wo_psum"], b + 1)
                tt(x_res[:, b, :], ps[:, b, :], x_res[:, b, :], ALU.add).then_inc(s["x1_done"], 1)
            layer_norm(1, lambda b: dve.wait_ge(s["x1_done"], b + 1))
            dve.wait_ge(s["soft_c"], 1)
            nc.vector.scalar_tensor_tensor(soft[:, 0], temp[:], 0.0, soft[:, 2], ALU.max, ALU.add).then_inc(s["soft_d"], 1)
            dve.wait_ge(s["kzero"], 1)
            for hg in range(C):
                dve.wait_ge(s["q2_evac"], hg + 1)
                for j in range(J):
                    rows = slice(j * HD, (j + 1) * HD)
                    nc.vector.tensor_copy(q_blocks[rows, hg::C, j, :],
                                          w_o[rows, hg, :].rearrange("p (b q) -> p b q", b=B)).then_inc(s["q2_blocks"], 1)
            for hg in range(C):
                dve.wait_ge(s["k2_psum"], hg + 1)
                for j in range(J):
                    rows = slice(j * HD, (j + 1) * HD)
                    nc.vector.tensor_copy(k_blocks[rows, hg::C, j, :],
                                          ps[rows, 4 + hg, :].rearrange("p (b q) -> p b q", b=B)).then_inc(s["k2_blocks"], 1)
            dve.wait_ge(s["pos_done"], 1)
            dve.wait_ge(s["attn_dve"], 3 * T)
            for n in range(P // 4):
                dve.wait_ge(s["rq_psum"], n + 1)
                pm = pos[:, 4 * n:4 * n + 4].rearrange("p (m o) -> p m o", o=1).broadcast_to([P, 4, B * H])
                tt(s_buf[:, 0, :, 4 * n:4 * n + 4].rearrange("p n m -> p m n"),
                   ps[:, n % 8, :].rearrange("p (m o n) -> p m o n", m=4, o=2)[:, :, 0, :], pm,
                   ALU.add).then_inc(s["rq_evac"], 1)
            dve.wait_ge(s["rq_evac"], P // 4)

            def keys(t, b):
                return t[:, b * H:(b + 1) * H].rearrange("p (h o) -> p h o", o=1).broadcast_to([P, H, P])

            def row_sum(b, done):
                nc.vector.tensor_reduce(rsum[:, b * H:(b + 1) * H], s_buf[:, 0, b * H:(b + 1) * H, :], AX.X,
                                        ALU.add).then_inc(done, 1)

            for b in range(B):
                for hg in range(C):
                    g = b * C + hg
                    dve.wait_ge(s["lg_psum"], g + 1)
                    part = s_buf[:, 0, g * J:(g + 1) * J, :]
                    tt(part, ps[:, g % 8, :].rearrange("p (j m) -> p j m", j=J), part, ALU.add).then_inc(s["lg_done"], 1)
                dve.wait_ge(s["lg_done"], C * (b + 1))
                part = s_buf[:, 0, b * H:(b + 1) * H, :]
                nc.vector.tensor_reduce(rmax[:, b * H:(b + 1) * H], part, AX.X, ALU.max).then_inc(s["max2"], 1)
                if b < 2:
                    dve.wait_ge(s["max2"], b + 1)
                    tt(part, part, keys(rmax, b), ALU.subtract).then_inc(s["sub2_dve"], 1)
            for b in range(B):
                dve.wait_ge(s["exp2"], b + 1)
                row_sum(b, s["sum2"])
            dve.wait_ge(s["sum2"], B)
            nc.vector.reciprocal(rinv[:], rsum[:]).then_inc(s["rinv2"], 1)
            for g in range(1, G, 2):
                dve.wait_ge(s["at_psum"], g + 1)
                nc.vector.tensor_copy(probs_t[:, g, :, :], ps[:, g % 4, :].rearrange("p (j q) -> p j q", j=J)).then_inc(s["at_dve"], 1)
            dve.wait_ge(s["ot2_evac"], B)
            dve.wait_ge(s["ev2"], 4)
            ev_part = ps[:, 0:4, :].rearrange("p a n -> p (a n)").rearrange("p (q g j) -> p g q j", g=G, j=J)
            out_t = s_buf[:, 1, 0:G, :].rearrange("p g (q i) -> p g q i", i=4)
            for i in range(4):
                for j in range(J):
                    dst = out_t[j * HD:(j + 1) * HD, :, :, i]
                    tt(dst, ev_part[i * HD:(i + 1) * HD, :, :, j], dst, ALU.add).then_inc(s["ot2_done"], 1)
            dve.wait_ge(s["rinv2"], 1)
            for b in range(B):
                dve.wait_ge(s["back_psum"], b + 1)
                tmp = s_buf[:, 1, 16 + 4 * b:20 + 4 * b, :].rearrange("p a n -> p (a n)")
                r = rinv[:, b * H:(b + 1) * H].rearrange("p (h o) -> p h o", o=1).broadcast_to([P, H, HD])
                tt(tmp.rearrange("p (h d) -> p h d", h=H), ps[:, 4 + b, :].rearrange("p (h d) -> p h d", h=H), r,
                   ALU.mult).then_inc(s["back_mul"], 1)
            for b in range(B):
                dve.wait_ge(s["back_mul"], b + 1)
                tmp = s_buf[:, 1, 16 + 4 * b:20 + 4 * b, :].rearrange("p a n -> p (a n)")
                tt(x_res[:, b, :], x_res[:, b, :], tmp, ALU.add).then_inc(s["x2_done"], 1)
            dve.wait_ge(s["av2"], B)
            layer_norm(2, lambda b: dve.wait_ge(s["x2_done"], b + 1))

            dve.wait_ge(s["b3_in"], 16)
            q3 = s_buf[:, 1, 0:16, :].rearrange("p (b a) n -> p b (a n)", b=B)
            for b in range(B):
                dve.wait_ge(s["q3_psum"], b + 1)
                tt(q3[:, b, :], ps[:, 4 + b, :], bias3[:, 0, :], ALU.add).then_inc(s["q3_bias"], 1)
            for hg in range(C):
                dve.wait_ge(s["k3_psum"], hg + 1)
                for j in range(J):
                    rows = slice(j * HD, (j + 1) * HD)
                    nc.vector.tensor_scalar(k_blocks[rows, hg::C, j, :],
                                            ps[rows, hg, :].rearrange("p (b q) -> p b q", b=B),
                                            cols[rows, 2, hg:hg + 1], None, ALU.add).then_inc(s["k3_blocks"], 1)
            dve.wait_ge(s["q3_sq"], 1)
            sq = s_buf[:, 1, 16:32, :].rearrange("p a n -> p (a n)").rearrange("p (n d) -> p n d", d=HD)
            nc.vector.tensor_reduce(rsum[:], sq, AX.X, ALU.add).then_inc(s["q3_ss"], 1)
            for b in range(B):
                dve.wait_ge(s["v3_psum"], b + 1)
                tt(v_buf[:, 1, b, :], ps[:, 4 + b, :], bias3[:, 2, :], ALU.add).then_inc(s["v3_done"], 1)
            dve.wait_ge(s["q3_rt"], 1)
            nc.vector.reciprocal(rinv[:], rsum[:]).then_inc(s["q3_rn"], 1)
            dve.wait_ge(s["q3_rn"], 1)
            q3h = s_buf[:, 1, 0:16, :].rearrange("p a n -> p (a n)").rearrange("p (n d) -> p n d", d=HD)
            tt(q3h, q3h, rinv[:, :].rearrange("p (n o) -> p n o", o=1).broadcast_to([P, B * H, HD]),
               ALU.mult).then_inc(s["q3_a"], 1)
            dve.wait_ge(s["q3_a"], 1)
            tt(q3, q3, bias3[:, 1:2, :].broadcast_to([P, B, D]), ALU.add).then_inc(s["q3_b"], 1)
            dve.wait_ge(s["q3_b"], 1)
            dve.wait_ge(s["soft_d"], 1)
            for b in range(B):
                dst = q3h[:, b * H:(b + 1) * H, :]
                last = tt(dst, dst, soft[:, 0, :].rearrange("p (h o) -> p h o", o=1).broadcast_to([P, H, HD]), ALU.mult)
            last.then_inc(s["q3_done"], 1)
            for b in range(B):
                dve.wait_ge(s["lg3_psum"], C * (b + 1))
                bank = 4 * (b % 2)
                part = ps[:, bank:bank + 4, :].rearrange("p a n -> p (a n)").rearrange("p (h m) -> p h m", m=P)
                nc.vector.tensor_reduce(rmax[:, b * H:(b + 1) * H], part, AX.X, ALU.max).then_inc(s["max3"], 1)
                dve.wait_ge(s["max3"], b + 1)
                tt(s_buf[:, 0, b * H:(b + 1) * H, :], part, keys(rmax, b), ALU.subtract).then_inc(s["sub3"], 1)
            for b in (2, 3, 0, 1):
                n = (2, 3, 0, 1).index(b)
                dve.wait_ge(s["exp3"], b + 1)
                row_sum(b, s["sum3"])
                dve.wait_ge(s["sum3"], n + 1)
                nc.vector.reciprocal(rinv[:, b * H:(b + 1) * H], rsum[:, b * H:(b + 1) * H]).then_inc(s["rinv3"], 1)
            for b in range(2):
                dve.wait_ge(s["rinv3"], 3 + b)
                part = s_buf[:, 0, b * H:(b + 1) * H, :]
                tt(part, part, keys(rinv, b), ALU.mult).then_inc(s["nrm3_dve"], 1)
            for g in range(1, G, 2):
                dve.wait_ge(s["at3_psum"], g + 1)
                nc.vector.tensor_copy(probs_t[:, g, :, :], ps[:, g % 4, :].rearrange("p (j q) -> p j q", j=J)).then_inc(s["at3_dve"], 1)
            for b in range(B):
                dve.wait_ge(s["g_psum"], b + 1)
                tt(gate[:, b, :], ps[:, 4 + b, 0:NG], b_gate[:], ALU.add).then_inc(s["g_bias"], 1)
            dve.wait_ge(s["g_bias"], B)
            routed, shared = gate[:, :, 0:NR], gate[:, :, NR:NG]
            nc.vector.tensor_reduce(gtmp[:, :, 0], routed, AX.X, ALU.max).then_inc(s["g_max"], 1)
            nc.vector.tensor_reduce(gtmp[:, :, 1], shared, AX.X, ALU.max).then_inc(s["g_max"], 1)
            dve.wait_ge(s["g_max"], 2)
            tt(routed, routed, gtmp[:, :, 0:1].broadcast_to([P, B, NR]), ALU.subtract).then_inc(s["g_sub"], 1)
            tt(shared, shared, gtmp[:, :, 1:2].broadcast_to([P, B, 2]), ALU.subtract).then_inc(s["g_sub"], 1)
            dve.wait_ge(s["g_exp"], 1)
            for b in range(B):
                nc.vector.max(top8[:, b, :], gate[:, b, 0:NR]).then_inc(s["g_top"], 1)
            nc.vector.tensor_reduce(gtmp[:, :, 2], routed, AX.X, ALU.add).then_inc(s["g_c1"], 1)
            nc.vector.tensor_reduce(gtmp[:, :, 3], shared, AX.X, ALU.add).then_inc(s["g_c1"], 1)
            dve.wait_ge(s["g_top"], B)
            nc.vector.tensor_reduce(gtmp[:, :, 4], top8[:, :, 0:3], AX.X, ALU.add).then_inc(s["g_c1"], 1)
            dve.wait_ge(s["g_c1"], 3)
            nc.vector.reciprocal(gtmp[:, :, 2:4], gtmp[:, :, 2:4]).then_inc(s["g_c2"], 1)
            dve.wait_ge(s["g_c2"], 1)
            tt(shared, shared, gtmp[:, :, 3:4].broadcast_to([P, B, 2]), ALU.mult).then_inc(s["g_c3"], 1)
            nc.vector.scalar_tensor_tensor(gtmp[:, :, 4], gtmp[:, :, 4], 3.0, gtmp[:, :, 2], ALU.mult,
                                           ALU.mult).then_inc(s["g_c3"], 1)
            dve.wait_ge(s["g_c3"], 2)
            tt(gtmp[:, :, 5], gate[:, :, NR], gate[:, :, NR + 1], ALU.add).then_inc(s["g_c4"], 1)
            nc.vector.scalar_tensor_tensor(gtmp[:, :, 6], gate[:, :, NR + 1], 2.0, gtmp[:, :, 4], ALU.mult,
                                           ALU.mult).then_inc(s["g_c4"], 1)
            dve.wait_ge(s["g_c4"], 2)
            nc.vector.scalar_tensor_tensor(gtmp[:, :, 7], gate[:, :, NR], 2.0, gtmp[:, :, 5], ALU.mult,
                                           ALU.mult).then_inc(s["g_c5"], 1)
            dve.wait_ge(s["g_c5"], 1)
            tt(rstd[:], gtmp[:, :, 6], gtmp[:, :, 7], ALU.add).then_inc(s["g_c6"], 1)
            dve.wait_ge(s["g_c6"], 1)
            dve.wait_ge(s["xp_done"], 1)
            for b in range(B):
                dve.wait_ge(s["y_psum"], b + 1)
                nc.vector.scalar_tensor_tensor(x_res[:, b, :], ps[:, b, :], rstd[:, b:b + 1], x_res[:, b, :],
                                               ALU.mult, ALU.add).then_inc(s["fin_done"], 1)


def kernel(**inputs):
    import concourse.bacc as bacc
    from concourse.bass_utils import run_bass_kernel_spmd

    f = {k: np.asarray(v) for k, v in inputs.items()}

    def chunks(w):
        return w.reshape(C, P, -1).transpose(1, 0, 2)

    rel = np.clip(np.arange(P)[:, None] - np.arange(P)[None, :], -64, 64) + 64
    span = np.arange(2 * P - 1)
    arrays = {
        "x": f["x"],
        "ctxT": f["ctx_1024"].reshape(B, T, P, C, P).transpose(1, 4, 3, 0, 2).reshape(T, P, C, D),
        "Wq1": chunks(f["L0_xattn_Wq"]), "Wk1": chunks(f["L0_xattn_Wk"]), "Wv1": chunks(f["L0_xattn_Wv"]),
        "Wo1": chunks(f["L0_xattn_Wo"]), "bv1": f["L0_xattn_bv"], "bo1": f["L0_xattn_bo"],
        "cols": np.stack([f["L0_xattn_bq"], f["L0_xattn_bk"], f["L0_ffn_bk"]]).reshape(3, C, P).transpose(2, 0, 1),
        "Wq2": chunks(f["L0_attn_Wq"]), "Wk2": chunks(f["L0_attn_Wk"]), "Wv2": chunks(f["L0_attn_Wv"]),
        "EqRel": f["L0_attn_Eq"][rel], "EkRel": f["L0_attn_Ek"][rel],
        "EvRel": f["L0_attn_Ev"][rel.T],
        "EkTab": np.tile(f["L0_attn_Ek"][np.clip(127 - span, -64, 64) + 64].T, (J, 1)),
        "EqTab": np.tile(f["L0_attn_Eq"][np.clip(span - 127, -64, 64) + 64].T, (J, 1)),
        "Wq3": chunks(f["L0_ffn_Wq"].T), "Wk3": chunks(f["L0_ffn_Wk"].T), "Wv3": chunks(f["L0_ffn_Wv"].T),
        "Wp3": chunks(f["L0_ffn_Wp"].T),
        "Wg": chunks(np.concatenate([f["L0_ffn_Wr"], f["L0_ffn_Ws"]]).T),
        "bg": np.concatenate([f["L0_ffn_br"], f["L0_ffn_bs"]]),
        "temp": f["L0_ffn_temperature"].reshape(H),
        "bias3": np.stack([f["L0_ffn_bq"], f["L0_ffn_query_embedding"].reshape(D), f["L0_ffn_bv"], f["L0_ffn_bp"]]),
    }
    arrays = {k: np.ascontiguousarray(v) for k, v in arrays.items()}
    nc = bacc.Bacc("TRN2", target_bir_lowering=False, num_devices=1)
    aps = {k: nc.dram_tensor("in_" + k, v.shape, mybir.dt.from_np(v.dtype), kind="ExternalInput").ap()
           for k, v in arrays.items()}
    out = nc.dram_tensor("out", (B, P, D), F32, kind="ExternalOutput").ap()
    program(nc, aps, out)
    r = run_bass_kernel_spmd(nc, [{"in_" + k: v for k, v in arrays.items()}], core_ids=[0])
    return r.results[0]["out"]
```

```python
from contextlib import ExitStack

import concourse.bass as bass
import numpy as np
from concourse import mybir

F32 = mybir.dt.float32
F32R = mybir.dt.float32r
BF16 = mybir.dt.bfloat16
ACT = mybir.ActivationFunctionType
ALU = mybir.AluOpType
AX = mybir.AxisListType

P = 128
B = 4
D = 512
C = D // P
H = 16
HD = D // H
J = P // HD
G = B * C
SK = 2048
T = SK // P
NR = 15
NG = NR + 2
EPS = 1e-5
SCALE = float(HD) ** -0.5


def program(nc, a, out):
    with ExitStack() as ctx:
        def sb(name, shape, dt=F32):
            return ctx.enter_context(nc.sbuf_tensor(name, shape, dt))

        def sem(name):
            return ctx.enter_context(nc.semaphore(name))

        x_res = sb("x_res", [P, B, D])
        blocks = sb("blocks", [P, G, J, P])
        s_buf = sb("s_buf", [P, 2, B * H, P])
        raw = sb("raw", [P, C, D])
        x_hi = sb("x_hi", [P, C, D], F32R)
        x_lo = sb("x_lo", [P, C, D], F32R)
        w_hi = sb("w_hi", [P, 2, C, D], F32R)
        w_lo = sb("w_lo", [P, 2, C, D], F32R)
        k_t = sb("k_t", [P, C, D])
        v_buf = sb("v_buf", [P, 2, B, D])
        extra = sb("extra", [P, 4096])
        pool_tmp = extra[:, 0:2048]
        bv_all = extra[:, 2048:2560]
        bo_all = extra[:, 2560:3072]
        m_part = extra[:, 3072:3584].rearrange("p (b q) -> p b q", b=B)
        z_part = extra[:, 3584:3968].rearrange("p (n q) -> p n q", n=3)
        ev_rel = extra[:, :].rearrange("p (l d) -> p l d", d=HD)
        bias3 = extra[:, 0:2048].rearrange("p (n e) -> p n e", n=4)
        ident = sb("ident", [P, P])
        m_all = sb("m_all", [P, P])
        r_all = sb("r_all", [P, P])
        ek_parts = sb("ek_parts", [3 * HD, 3, 2 * P], BF16)
        eq_parts = sb("eq_parts", [3 * HD, 3, 2 * P], BF16)
        pos = sb("pos", [P, P])
        cols = sb("cols", [P, 3, C])
        stats = sb("stats", [P, B, 6])
        mean_var = sb("mean_var", [P, B, 2])
        rstd = sb("rstd", [P, B])
        temp = sb("temp", [P, H])
        soft = sb("soft", [P, 3, H])
        rmax = sb("rmax", [P, B * H])
        rsum = sb("rsum", [P, B * H])
        rinv = sb("rinv", [P, B * H])
        w_gate = sb("w_gate", [P, C, NG])
        b_gate = sb("b_gate", [P, NG])
        gate = sb("gate", [P, B, NG])
        gtmp = sb("gtmp", [P, B, 8])
        top8 = sb("top8", [P, B, 8])
        ps = ctx.enter_context(nc.psum_tensor("ps", [P, 8, 512], F32))

        def half(n, lo, hi):
            return s_buf[:, n, lo:hi, :].rearrange("p (c a) q -> p c (a q)", a=4)

        def as_bf16(t, n):
            return t.rearrange("p a q -> p (a q)").bitcast(BF16)[:, 0:n]

        y_ln0, y_ln = v_buf[:, 1], v_buf[:, 0]
        x_t0, wq_raw, wk_raw, wv_raw = (half(0, 16 * n, 16 * n + 16) for n in range(4))
        tab_raw = k_t[0:3 * HD, 0:2, 0:2 * P]
        eq_rel = s_buf[:, 1, 0:32, :].rearrange("p h (m d) -> p (h m) d", d=HD)
        ek_rel = s_buf[:, 1, 32:64, :].rearrange("p h (m d) -> p (h m) d", d=HD)
        q_parts = as_bf16(s_buf[:, 1, 0:24, :], 3 * 2048).rearrange("p (r c n) -> p r c n", r=3, c=C)
        q_rest = half(1, 32, 48)
        k_parts = as_bf16(s_buf[:, 0, 32:56, :], 3 * 2048).rearrange("p (r c n) -> p r c n", r=3, c=C)
        q_pack = as_bf16(s_buf[:, 0, 0:32, :], 8192)
        k_pack = extra[:, :].bitcast(BF16)
        probs_t = s_buf[:, 1].rearrange("p (g j) q -> p g j q", j=J)
        lg = s_buf[:, 0].rearrange("p (n b) q -> p n b q", b=B)

        names = """x_in wq_in wk_in wv_in cols_in bv_in bo_in tab_in ctx_in ctx_hi ctx_lo wkv_hi wkv_lo wraw_in wsplit_hi wsplit_lo
            tab_h tab_r tab_m tab_l x_hi_done x_lo_done rel_in small_in
            ident_done qzero stats_done mv_done var_done std_done rstd_done ln_done tr_done tr_evac q_psum q_evac xb_done
            pos_mul pos_done
            kv_psum kv_evac v_ready s_psum s_evac max_done m_ready sub_done exp_done
            sum_dve zadd zmore zpool z_done r_ready attn_dve attn_pool av_done
            ot_evac wo_psum x1_done
            ev_in qpack_in kpack_in qh qr qm ql kf_evac kh kr km kl
            q2_psum q2_evac q2_blocks k2_psum k2_blocks v2_psum v2_evac
            rk_psum rk_evac rq_psum rq_evac lg_psum lg_done max2 sub2_dve sub2_pool exp2 sum2 rinv2
            at_psum at_act at_dve av2 ev2 ot2_evac ot2_done back_psum back_mul x2_done
            soft_a soft_b soft_c soft_d soft_e
            b3_in xp_done
            q3_psum q3_bias q3_sq q3_ss q3_rt q3_rn q3_a q3_b q3_done q3t_psum q3t_evac k3_psum k3_blocks v3_psum v3_done
            lg3_psum max3 sub3 exp3 sum3 rinv3 nrm3_dve nrm3_pool at3_psum at3_act at3_dve av3 ot3_evac ot3_hi ot3_lo
            g_psum g_bias g_max g_sub g_exp g_top g_c1 g_c2 g_c3 g_c4 g_c5 g_c6 y_psum fin_done out_done""".split()
        s = {n: sem(n) for n in names}

        block = ctx.enter_context(nc.Block())

        def schedule(eng, first, stage, last):
            first()
            stage(0, 0)
            with eng.Fori(0, (T - 4) // 2) as i:
                stage(2 * i + 1, 1)
                stage(2 * i + 2, 0)
            stage(T - 3, 1)
            stage(T - 2, 0)
            last()

        WEIGHTS = [("Wo1", "kv_psum", 8 * T), ("Wq2", "kv_psum", 8 * T), ("Wk2", "wo_psum", B), ("Wv2", "q2_psum", C),
                   ("Wq3", "k2_psum", C), ("Wk3", "v2_psum", B), ("Wv3", "q3_psum", B), ("Wp3", "k3_psum", C)]

        @block.sync
        def _(sp):
            def load(dst, src, name):
                sp.dma_start(dst, src).then_inc(s[name], 16)

            load(wk_raw, a["Wk1"], "wk_in")
            load(raw[:], a["ctxT"][0], "ctx_in")
            load(wv_raw, a["Wv1"], "wv_in")
            load(x_res[:], a["x"].rearrange("b q e -> q b e"), "x_in")
            load(tab_raw[:, 0, 0:2 * P - 1], a["EkTab"], "tab_in")
            load(tab_raw[:, 1, 0:2 * P - 1], a["EqTab"], "tab_in")
            load(cols[:], a["cols"], "cols_in")
            load(wq_raw, a["Wq1"], "wq_in")
            load(bv_all, a["bv1"].partition_broadcast(P), "bv_in")
            load(bo_all, a["bo1"].partition_broadcast(P), "bo_in")
            load(eq_rel, a["EqRel"], "rel_in")
            load(ek_rel, a["EkRel"], "rel_in")

            def ctx_load(t):
                sp.wait_ge(s["ctx_hi"], C * t)
                sp.wait_ge(s["ctx_lo"], C * t)
                load(raw[:], a["ctxT"][t], "ctx_in")

            ctx_load(1)
            load(temp[:], a["temp"].partition_broadcast(P), "small_in")
            load(w_gate[:], a["Wg"], "small_in")
            load(b_gate[:], a["bg"].partition_broadcast(P), "small_in")
            with sp.Fori(2, T) as t:
                ctx_load(t)

            def weight_load(n):
                if n == 0:
                    sp.wait_ge(s["ctx_hi"], C * T)
                    sp.wait_ge(s["ctx_lo"], C * T)
                else:
                    sp.wait_ge(s["wsplit_lo"], n)
                load(raw[:], a[WEIGHTS[n][0]], "wraw_in")

            def pack(dst, parts, done, landed):
                sp.wait_ge(s[done], C)
                for r in range(3):
                    for j in range(J):
                        load(dst[r * HD:(r + 1) * HD, j * 2048:(j + 1) * 2048],
                             parts[j * HD:(j + 1) * HD, r].rearrange("p c n -> p (c n)"), landed)

            for n in range(4):
                weight_load(n)
            pack(q_pack, q_parts, "ql", "qpack_in")
            weight_load(4)
            pack(k_pack, k_parts, "kl", "kpack_in")
            weight_load(5)
            sp.wait_ge(s["rq_psum"], 16)
            load(ev_rel, a["EvRel"], "ev_in")
            weight_load(6)
            sp.wait_ge(s["ev2"], 4)
            load(bias3, a["bias3"].rearrange("(o n) e -> o n e", o=1).broadcast_to([P, 4, D]), "b3_in")
            weight_load(7)
            for b in range(B):
                sp.wait_ge(s["fin_done"], b + 1)
                sp.dma_start(out[b], x_res[:, b, :]).then_inc(s["out_done"], 16)
            sp.wait_ge(s["out_done"], 16 * B)

        @block.tensor
        def _(pe):
            mm = nc.tensor.matmul

            PARTS = ((0, 0), (0, 1), (1, 0))
            x_parts, w_parts = (x_hi, x_lo), (w_hi, w_lo)

            def transposes(y, banks, k):
                for c in range(C):
                    for b in range(B):
                        if c == 0:
                            pe.wait_ge(s["ln_done"], B * k + b + 1)
                        last = nc.tensor.transpose(ps[:, banks + c, b * P:(b + 1) * P], y[:, b, c * P:(c + 1) * P], ident[:])
                    last.then_inc(s["tr_done"], 1)

            def proj_t(slot, bank, done, hg):
                for n, (u, v) in enumerate(PARTS):
                    for c in range(C):
                        last = mm(ps[:, bank, :], w_parts[v][:, slot, c, hg * P:(hg + 1) * P], x_parts[u][:, c, :],
                                  start=n + c == 0, stop=n == 2 and c == C - 1)
                last.then_inc(done, 1)

            def proj_n(slot, bank, done, b):
                for n, (u, v) in enumerate(PARTS):
                    for c in range(C):
                        last = mm(ps[:, bank, :], x_parts[u][:, c, b * P:(b + 1) * P], w_parts[v][:, slot, c, :],
                                  start=n + c == 0, stop=n == 2 and c == C - 1)
                last.then_inc(done, 1)

            def out_proj(slot, bank, done, b):
                for n, (u, v) in enumerate(PARTS):
                    for c in range(C):
                        last = mm(ps[:, bank, :], x_parts[u][:, b, c * P:(c + 1) * P], w_parts[v][:, slot, c, :],
                                  start=n + c == 0, stop=n == 2 and c == C - 1)
                last.then_inc(done, 1)

            def weight_ready(n):
                pe.wait_ge(s["wsplit_lo"], n + 1)

            def project(t):
                pe.wait_ge(s["ctx_lo"], C * t + C)
                for n in range(8):
                    if n >= 2 or not (isinstance(t, int) and t == 0):
                        pe.wait_ge(s["kv_evac"], 8 * t + n - 1)
                    if n < 4:
                        proj_t(0, n % 2, s["kv_psum"], n)
                    else:
                        proj_n(1, n % 2, s["kv_psum"], n - 4)

            def score(t):
                for g in range(G):
                    b, hg = divmod(g, C)
                    if g == 0:
                        pe.wait_ge(s["kv_evac"], 8 * t + 4)
                    if g >= 2 or not (isinstance(t, int) and t == 0):
                        pe.wait_ge(s["s_evac"], 16 * t + g - 1)
                    mm(ps[:, 2 + g % 2, :], k_t[:, hg, b * P:(b + 1) * P],
                       blocks[:, g].rearrange("p j q -> p (j q)"), start=True, stop=True).then_inc(s["s_psum"], 1)

            def attend(t, p, first=False, final=False):
                for b in range(B):
                    pe.wait_ge(s["v_ready"], B * t + b + 1)
                    if b < 3:
                        pe.wait_ge(s["attn_dve"], 3 * t + b + 1)
                    else:
                        pe.wait_ge(s["attn_pool"], t + 1)
                    for hg in range(C):
                        for j in range(J):
                            h = hg * J + j
                            last = mm(ps[j * HD:(j + 1) * HD, 4 + b, hg * P:(hg + 1) * P],
                                      v_buf[:, p, b, h * HD:(h + 1) * HD], s_buf[:, p, b * H + h, :],
                                      start=first and hg == 0, stop=final and hg == C - 1, skip_group_check=True)
                    last.then_inc(s["av_done"], 1)

            def first():
                pe.wait_ge(s["wkv_lo"], 2)
                project(0)
                pe.wait_ge(s["ident_done"], 2)
                transposes(y_ln0, 4, 0)
                pe.wait_ge(s["wq_in"], 16)
                pe.wait_ge(s["x_hi_done"], C)
                for hg in range(C):
                    for c in range(C):
                        last = mm(ps[:, 4 + hg, :], wq_raw[:, c, hg * P:(hg + 1) * P], x_t0[:, c, :],
                                  start=c == 0, stop=c == C - 1)
                    last.then_inc(s["q_psum"], 1)
                pe.wait_ge(s["q_evac"], 16)
                score(0)

            def stage(t, p):
                project(t + 1)
                score(t + 1)
                attend(t, p, first=isinstance(t, int) and t == 0)

            def last():
                attend(T - 1, 1, final=True)

            schedule(pe, first, stage, last)

            weight_ready(0)
            for b in range(B):
                pe.wait_ge(s["x_lo_done"], b + 1)
                out_proj(0, b, s["wo_psum"], b)

            transposes(y_ln, 4, 1)
            weight_ready(1)
            pe.wait_ge(s["x_lo_done"], 2 * C)
            for hg in range(C):
                pe.wait_ge(s["x1_done"], hg + 1)
                proj_t(1, hg, s["q2_psum"], hg)
            weight_ready(2)
            for hg in range(C):
                proj_t(0, 4 + hg, s["k2_psum"], hg)
            weight_ready(3)
            for b in range(B):
                pe.wait_ge(s["q2_evac"], b + 1)
                proj_n(1, b, s["v2_psum"], b)

            def relative(parts, pack, psum_done, drained):
                for n in range(16):
                    drained(n)
                    for i in range(8):
                        r = 8 * n + i
                        rows = pack[0:3 * HD, :].rearrange("p (n q) -> p n q", q=P)[:, :, r]
                        for u in range(3):
                            last = mm(ps[:, n % 8, i * 64:(i + 1) * 64], parts[:, u, P - 1 - r:2 * P - 1 - r], rows,
                                      start=u == 0, stop=u == 2, skip_group_check=True)
                    last.then_inc(psum_done, 1)

            def rk_free(n):
                if n < 4:
                    pe.wait_ge(s["v2_evac"], n + 1)
                elif n < 8:
                    pe.wait_ge(s["kf_evac"], n - 3)
                else:
                    pe.wait_ge(s["rk_evac"], n - 7)

            def rq_free(n):
                if n < 8:
                    pe.wait_ge(s["rk_evac"], 8 + n + 1)
                else:
                    pe.wait_ge(s["rq_evac"], n - 7)

            pe.wait_ge(s["tab_l"], 2)
            pe.wait_ge(s["qpack_in"], 16 * 12)
            relative(ek_parts, q_pack, s["rk_psum"], rk_free)
            pe.wait_ge(s["kpack_in"], 16 * 12)
            relative(eq_parts, k_pack, s["rq_psum"], rq_free)
            pe.wait_ge(s["k2_blocks"], 16)
            for g in range(G):
                b, hg = divmod(g, C)
                if g < 8:
                    pe.wait_ge(s["rq_evac"], 8 + g + 1)
                else:
                    pe.wait_ge(s["lg_done"], g - 7)
                for j in range(J):
                    mm(ps[:, g % 8, j * P:(j + 1) * P], s_buf[:, 1, (j * C + hg) * B + b, :], ident[:],
                       start=j == 0, stop=False, is_transpose=True, skip_group_check=True)
                mm(ps[:, g % 8, :], k_t[:, hg, b * P:(b + 1) * P], blocks[:, g].rearrange("p j m -> p (j m)"),
                   start=False, stop=True, skip_group_check=True).then_inc(s["lg_psum"], 1)
            for g in range(G):
                if g < 4:
                    pe.wait_ge(s["lg_done"], G)
                else:
                    pe.wait_ge(s["at_act"], (g - 4) // 2 + 1) if g % 2 == 0 else pe.wait_ge(s["at_dve"], (g - 4) // 2 + 1)
                pe.wait_ge(s["exp2"], g // C + 1)
                b, hg = divmod(g, C)
                for j in range(J):
                    last = nc.tensor.transpose(ps[:, g % 4, j * P:(j + 1) * P], lg[:, j * C + hg, b, :], ident[:])
                last.then_inc(s["at_psum"], 1)
            for g in range(G):
                b, hg = divmod(g, C)
                if g % 2 == 0:
                    pe.wait_ge(s["at_act"], g // 2 + 1)
                else:
                    pe.wait_ge(s["at_dve"], g // 2 + 1)
                for j in range(J):
                    h = hg * J + j
                    last = mm(ps[j * HD:(j + 1) * HD, 4 + b, hg * P:(hg + 1) * P], v_buf[:, 1, b, h * HD:(h + 1) * HD],
                              probs_t[:, g, j, :], start=hg == 0, stop=hg == C - 1, skip_group_check=True)
                if hg == C - 1:
                    last.then_inc(s["av2"], 1)
            pe.wait_ge(s["ev_in"], 16)
            for bank in range(4):
                for n in range(32):
                    l, i = bank * 32 + n, n % 4
                    last = mm(ps[i * HD:(i + 1) * HD, bank, n // 4 * 64:(n // 4 + 1) * 64], ev_rel[:, l, :],
                              probs_t[:, :, :, l].rearrange("p g j -> p (g j)"), start=n < 4, stop=n >= 28, skip_group_check=True)
                last.then_inc(s["ev2"], 1)
            for b in range(B):
                pe.wait_ge(s["ot2_done"], 16)
                for hg in range(C):
                    last = nc.tensor.transpose(ps[:, 4 + b, hg * P:(hg + 1) * P], k_t[:, b, hg * P:(hg + 1) * P], ident[:])
                last.then_inc(s["back_psum"], 1)

            transposes(y_ln, 0, 2)
            pe.wait_ge(s["x_lo_done"], 3 * C)
            weight_ready(4)
            for b in range(B):
                pe.wait_ge(s["back_mul"], b + 1)
                proj_n(0, 4 + b, s["q3_psum"], b)
            weight_ready(5)
            for hg in range(C):
                proj_t(1, hg, s["k3_psum"], hg)
            weight_ready(6)
            for b in range(B):
                pe.wait_ge(s["q3_bias"], b + 1)
                proj_n(0, 4 + b, s["v3_psum"], b)
            for c in range(C):
                pe.wait_ge(s["k3_blocks"], 4 * c + 4)
                for b in range(B):
                    pe.wait_ge(s["q3_done"], 1)
                    last = nc.tensor.transpose(ps[:, c, b * P:(b + 1) * P], s_buf[:, 1, b * C + c, :], ident[:])
                last.then_inc(s["q3t_psum"], 1)
            pe.wait_ge(s["q3t_evac"], C)
            for g in range(G):
                b, hg = divmod(g, C)
                if b == 1:
                    pe.wait_ge(s["v3_done"], B)
                if b >= 2:
                    pe.wait_ge(s["sub3"], b - 1)
                mm(ps[:, 4 * (b % 2) + hg, :], s_buf[:, 1, 32 + 4 * hg + b, :],
                   blocks[:, g].rearrange("p j m -> p (j m)"), start=True, stop=True).then_inc(s["lg3_psum"], 1)
            for g in range(G):
                if g < 4:
                    pe.wait_ge(s["sub3"], B)
                else:
                    pe.wait_ge(s["at3_act"] if g % 2 == 0 else s["at3_dve"], (g - 4) // 2 + 1)
                if g // C < 2:
                    pe.wait_ge(s["nrm3_dve"], g // C + 1)
                else:
                    pe.wait_ge(s["nrm3_pool"], g // C - 1)
                for j in range(J):
                    last = nc.tensor.transpose(ps[:, g % 4, j * P:(j + 1) * P], s_buf[:, 0, g * J + j, :], ident[:])
                last.then_inc(s["at3_psum"], 1)
            for g in range(G):
                b, hg = divmod(g, C)
                pe.wait_ge(s["at3_act"] if g % 2 == 0 else s["at3_dve"], g // 2 + 1)
                for j in range(J):
                    h = hg * J + j
                    last = mm(ps[j * HD:(j + 1) * HD, 4 + b, hg * P:(hg + 1) * P], v_buf[:, 1, b, h * HD:(h + 1) * HD],
                              probs_t[:, g, j, :], start=hg == 0, stop=hg == C - 1, skip_group_check=True)
                if hg == C - 1:
                    last.then_inc(s["av3"], 1)
            pe.wait_ge(s["small_in"], 48)
            for b in range(B):
                pe.wait_ge(s["ot3_evac"], b + 1)
                pe.wait_ge(s["ot3_hi"], b + 1)
                for hg in range(C):
                    last = mm(ps[:, 4 + b, 0:NG], k_t[:, b, hg * P:(hg + 1) * P], w_gate[:, hg, :],
                              start=hg == 0, stop=hg == C - 1)
                last.then_inc(s["g_psum"], 1)
            weight_ready(7)
            for b in range(B):
                pe.wait_ge(s["ot3_lo"], b + 1)
                out_proj(1, b, s["y_psum"], b)

        @block.scalar
        def _(act):
            copy = nc.scalar.copy

            def ln_std(k):
                act.wait_ge(s["var_done"], k + 1)
                nc.scalar.activation(rstd[:], rstd[:], ACT.Sqrt).then_inc(s["std_done"], 1)

            def weight_hi(n):
                act.wait_ge(s["wraw_in"], 16 * (n + 1))
                act.wait_ge(s[WEIGHTS[n][1]], WEIGHTS[n][2])
                copy(w_hi[:, n % 2], raw[:]).then_inc(s["wsplit_hi"], 1)

            def ctx_split(t, c):
                if c == 0:
                    act.wait_ge(s["ctx_in"], 16 * t + 16)
                    if not (isinstance(t, int) and t == 0):
                        act.wait_ge(s["kv_psum"], 8 * t)
                copy(x_hi[:, c, :], raw[:, c, :]).then_inc(s["ctx_hi"], 1)

            def kv_copy(t, p, n):
                act.wait_ge(s["kv_psum"], 8 * t + n + 1)
                if n < 4:
                    if not (isinstance(t, int) and t == 0):
                        act.wait_ge(s["s_psum"], 16 * t)
                    nc.scalar.activation(k_t[:, n, :], ps[:, n % 2, :], ACT.Identity,
                                         bias=cols[:, 1, n:n + 1]).then_inc(s["kv_evac"], 1)
                else:
                    if not (isinstance(t, int) and t <= 1):
                        act.wait_ge(s["av_done"], 4 * (t - 1))
                    copy(v_buf[:, p, n - 4, :], ps[:, n % 2, :]).then_inc(s["kv_evac"], 1)

            def s_copy(t, p, split=True):
                for g in range(G):
                    if g % C == 0 and not (isinstance(t, int) and t <= 1):
                        act.wait_ge(s["av_done"], 4 * (t - 2) + g // C + 1)
                    act.wait_ge(s["s_psum"], 16 * t + g + 1)
                    copy(s_buf[:, p, g * J:(g + 1) * J, :], ps[:, 2 + g % 2, :]).then_inc(s["s_evac"], 1)
                    if split and g in (1, 3, 5, 7):
                        ctx_split(t + 1, g // 2)

            def exp(t, p, b):
                act.wait_ge(s["sub_done"], 4 * t + b + 1)
                part = s_buf[:, p, b * H:(b + 1) * H, :]
                nc.scalar.activation(part, part, ACT.Exp).then_inc(s["exp_done"], 1)

            def first():
                act.wait_ge(s["wk_in"], 16)
                copy(w_hi[:, 0], wk_raw).then_inc(s["wkv_hi"], 1)
                for c in range(C):
                    ctx_split(0, c)
                act.wait_ge(s["wv_in"], 16)
                copy(w_hi[:, 1], wv_raw).then_inc(s["wkv_hi"], 1)
                ln_std(0)
                act.wait_ge(s["cols_in"], 16)
                act.wait_ge(s["tab_l"], 2)
                for n in range(8):
                    kv_copy(0, 0, n)
                for c in range(C):
                    act.wait_ge(s["tr_done"], c + 1)
                    copy(x_t0[:, c, :], ps[:, 4 + c, :]).then_inc(s["x_hi_done"], 1)
                s_copy(0, 0)

            def stage(t, p):
                for n in range(8):
                    kv_copy(t + 1, 1 - p, n)
                    if n in (1, 2, 3, 4):
                        exp(t, p, n - 1)
                if isinstance(t, int) and t == 0:
                    act.wait_ge(s["pos_done"], 1)
                s_copy(t + 1, 1 - p, split=not (isinstance(t, int) and t == T - 2))

            def last():
                weight_hi(0)
                for b in range(B):
                    exp(T - 1, 1, b)

            schedule(act, first, stage, last)

            def split_hi(c, bank):
                copy(x_hi[:, c, :], ps[:, bank, :]).then_inc(s["x_hi_done"], 1)

            for b in range(B):
                act.wait_ge(s["av_done"], B * (T - 1) + b + 1)
                split_hi(b, 4 + b)
            weight_hi(1)
            act.wait_ge(s["soft_a"], 1)
            nc.scalar.activation(soft[:, 1], soft[:, 0], ACT.Exp).then_inc(s["soft_b"], 1)
            act.wait_ge(s["soft_b"], 1)
            nc.scalar.activation(soft[:, 2], soft[:, 1], ACT.Ln, bias=1.0).then_inc(s["soft_c"], 1)

            weight_hi(2)
            ln_std(1)
            for c in range(C):
                act.wait_ge(s["tr_done"], C + c + 1)
                split_hi(c, 4 + c)
            for hg in range(C):
                act.wait_ge(s["q2_psum"], hg + 1)
                copy(k_t[:, hg, :], ps[:, hg, :]).then_inc(s["q2_evac"], 1)
                act.wait_ge(s["q2_evac"], hg + 1)
                copy(q_parts[:, 0, hg, :], k_t[:, hg, :]).then_inc(s["qh"], 1)
            for hg in range(C):
                act.wait_ge(s["qr"], hg + 1)
                copy(q_parts[:, 1, hg, :], q_rest[:, hg, :]).then_inc(s["qm"], 1)
            weight_hi(3)
            kf = v_buf[:, 0]
            for hg in range(C):
                act.wait_ge(s["k2_psum"], hg + 1)
                copy(kf[:, hg, :], ps[:, 4 + hg, :]).then_inc(s["kf_evac"], 1)
                act.wait_ge(s["kf_evac"], hg + 1)
                copy(k_parts[:, 0, hg, :], kf[:, hg, :]).then_inc(s["kh"], 1)
            for hg in range(C):
                act.wait_ge(s["kr"], hg + 1)
                copy(k_parts[:, 1, hg, :], kf[:, hg, :]).then_inc(s["km"], 1)
            weight_hi(4)
            for b in range(B):
                act.wait_ge(s["v2_psum"], b + 1)
                copy(v_buf[:, 1, b, :], ps[:, b, :]).then_inc(s["v2_evac"], 1)
            weight_hi(5)
            for n in range(16):
                act.wait_ge(s["rk_psum"], n + 1)
                copy(s_buf[:, 1, :, 8 * n:8 * n + 8].rearrange("p n l -> p l n"),
                     ps[:, n % 8, :].rearrange("p (l n) -> p l n", l=8)).then_inc(s["rk_evac"], 1)
            for b in range(B):
                act.wait_ge(s["sub2_dve"] if b < 2 else s["sub2_pool"], b % 2 + 1)
                part = lg[:, :, b, :]
                nc.scalar.activation(part, part, ACT.Exp, scale=SCALE).then_inc(s["exp2"], 1)
            for g in range(0, G, 2):
                act.wait_ge(s["at_psum"], g + 1)
                copy(probs_t[:, g, :, :], ps[:, g % 4, :]).then_inc(s["at_act"], 1)
            for b in range(B):
                act.wait_ge(s["av2"], b + 1)
                copy(k_t[:, b, :], ps[:, 4 + b, :]).then_inc(s["ot2_evac"], 1)

            ln_std(2)
            for c in range(C):
                act.wait_ge(s["tr_done"], 2 * C + c + 1)
                split_hi(c, c)
            act.wait_ge(s["q3_bias"], B)
            nc.scalar.activation(s_buf[:, 1, 16:32, :], s_buf[:, 1, 0:16, :], ACT.Square).then_inc(s["q3_sq"], 1)
            act.wait_ge(s["q3_ss"], 1)
            nc.scalar.activation(rsum[:], rsum[:], ACT.Sqrt).then_inc(s["q3_rt"], 1)
            weight_hi(6)
            weight_hi(7)
            for c in range(C):
                act.wait_ge(s["q3t_psum"], c + 1)
                copy(s_buf[:, 1, 32 + 4 * c:36 + 4 * c, :], ps[:, c, :]).then_inc(s["q3t_evac"], 1)
            for b in range(B):
                act.wait_ge(s["sub3"], b + 1)
                part = s_buf[:, 0, b * H:(b + 1) * H, :]
                nc.scalar.activation(part, part, ACT.Exp, scale=SCALE).then_inc(s["exp3"], 1)
            for g in range(0, G, 2):
                act.wait_ge(s["at3_psum"], g + 1)
                copy(probs_t[:, g, :, :], ps[:, g % 4, :]).then_inc(s["at3_act"], 1)
            for b in range(B):
                act.wait_ge(s["av3"], b + 1)
                copy(k_t[:, b, :], ps[:, 4 + b, :]).then_inc(s["ot3_evac"], 1)
                copy(x_hi[:, b, :], ps[:, 4 + b, :]).then_inc(s["ot3_hi"], 1)
            act.wait_ge(s["g_sub"], 2)
            nc.scalar.activation(gate[:], gate[:], ACT.Exp).then_inc(s["g_exp"], 1)

        @block.gpsimd
        def _(pool):
            pool.memset(ident[:], 0.0).then_inc(s["ident_done"], 1)
            pool.wait_ge(s["ident_done"], 1)
            pool.affine_select(out=ident[:], in_=ident[:], compare_op=ALU.not_equal, fill=1.0, base=0,
                               pattern=[[-1, P]], channel_multiplier=1).then_inc(s["ident_done"], 1)

            pool.wait_ge(s["tab_in"], 32)
            for n, parts in enumerate((ek_parts, eq_parts)):
                t = tab_raw[:, n, 0:2 * P - 1]
                u, v, w = (parts[:, r, 0:2 * P - 1] for r in range(3))
                pool.tensor_copy(u, t).then_inc(s["tab_h"], 1)
                pool.wait_ge(s["tab_h"], n + 1)
                pool.tensor_tensor(t, t, u, ALU.subtract).then_inc(s["tab_r"], 1)
                pool.wait_ge(s["tab_r"], n + 1)
                pool.tensor_copy(v, t).then_inc(s["tab_m"], 1)
                pool.wait_ge(s["tab_m"], n + 1)
                pool.tensor_tensor(w, t, v, ALU.subtract).then_inc(s["tab_l"], 1)
            pool.memset(blocks[:], 0.0).then_inc(s["qzero"], 1)
            pool.wait_ge(s["ln_done"], B)
            pool.wait_ge(s["bo_in"], 16)
            bo = bo_all.rearrange("p (o e) -> p o e", o=1).broadcast_to([P, B, D])
            pool.tensor_tensor(x_res[:], x_res[:], bo, ALU.add).then_inc(s["xb_done"], 1)
            pool.wait_ge(s["bv_in"], 16)

            def v_bias(t, p):
                for b in range(B):
                    pool.wait_ge(s["kv_evac"], 8 * t + 4 + b + 1)
                    pool.tensor_tensor(v_buf[:, p, b, :], v_buf[:, p, b, :], bv_all, ALU.add).then_inc(s["v_ready"], 1)

            def ctx_split(t):
                for c in range(C):
                    pool.wait_ge(s["ctx_hi"], C * t + c + 1)
                    pool.tensor_tensor(x_lo[:, c, :], raw[:, c, :], x_hi[:, c, :], ALU.subtract).then_inc(s["ctx_lo"], 1)

            def weight_lo(n):
                pool.wait_ge(s["wsplit_hi"], n + 1)
                pool.tensor_tensor(w_lo[:, n % 2], raw[:], w_hi[:, n % 2], ALU.subtract).then_inc(s["wsplit_lo"], 1)

            def sum_half(t, p):
                pool.wait_ge(s["exp_done"], 4 * t + 4)
                acc = pool_tmp.rearrange("p (h q) -> p h q", q=P)
                pool.tensor_tensor(acc, s_buf[:, p, 2 * H:3 * H, :], s_buf[:, p, 3 * H:4 * H, :],
                                   ALU.add).then_inc(s["zadd"], 1)
                for n, w in enumerate((8, 4, 2)):
                    pool.wait_ge(s["zadd"], 4 * t + n + 1)
                    pool.tensor_tensor(acc[:, 0:w], acc[:, 0:w], acc[:, w:2 * w], ALU.add).then_inc(s["zadd"], 1)
                pool.wait_ge(s["zadd"], 4 * t + 4)
                if not (isinstance(t, int) and t == 0):
                    pool.wait_ge(s["z_done"], 2 * t)
                pool.tensor_tensor(z_part[:, 2], acc[:, 0], acc[:, 1], ALU.add).then_inc(s["zpool"], 1)

            def normalise(t, p):
                pool.wait_ge(s["r_ready"], t + 1)
                part = s_buf[:, p, 3 * H:4 * H, :]
                r = r_all[:, :].rearrange("p (o q) -> p o q", o=1).broadcast_to([P, H, P])
                pool.tensor_tensor(part, part, r, ALU.mult).then_inc(s["attn_pool"], 1)

            def first():
                ctx_split(1)
                v_bias(0, 0)

            def stage(t, p):
                sum_half(t, p)
                normalise(t, p)
                if not (isinstance(t, int) and t == T - 2):
                    ctx_split(t + 2)
                v_bias(t + 1, 1 - p)

            def last():
                weight_lo(0)
                sum_half(T - 1, 1)
                normalise(T - 1, 1)

            schedule(pool, first, stage, last)

            for n in range(1, 6):
                weight_lo(n)
            for b in (2, 3):
                pool.wait_ge(s["max2"], b + 1)
                part = lg[:, :, b, :]
                m = rmax[:, b * H:(b + 1) * H].rearrange("p (h o) -> p h o", o=1).broadcast_to([P, H, P])
                pool.tensor_tensor(part, part, m, ALU.subtract).then_inc(s["sub2_pool"], 1)
            pool.wait_ge(s["ln_done"], 3 * B)
            pool.wait_ge(s["b3_in"], 16)
            bp = bias3[:, 3:4, :].broadcast_to([P, B, D])
            pool.tensor_tensor(x_res[:], x_res[:], bp, ALU.add).then_inc(s["xp_done"], 1)
            weight_lo(6)
            weight_lo(7)
            for b in (2, 3):
                pool.wait_ge(s["rinv3"], b + 1)
                part = s_buf[:, 0, b * H:(b + 1) * H, :]
                r = rinv[:, b * H:(b + 1) * H].rearrange("p (h o) -> p h o", o=1).broadcast_to([P, H, P])
                pool.tensor_tensor(part, part, r, ALU.mult).then_inc(s["nrm3_pool"], 1)

        @block.vector
        def _(dve):
            tt = nc.vector.tensor_tensor

            def layer_norm(k, ready):
                for b in range(B):
                    ready(b)
                    nc.vector.bn_stats(stats[:, b, :], x_res[:, b, :]).then_inc(s["stats_done"], 1)
                for b in range(B):
                    dve.wait_ge(s["stats_done"], B * k + b + 1)
                    nc.vector.bn_aggr(mean_var[:, b, :], stats[:, b, :]).then_inc(s["mv_done"], 1)
                dve.wait_ge(s["mv_done"], B * (k + 1))
                nc.vector.tensor_scalar(rstd[:], mean_var[:, :, 1], EPS, None, ALU.add).then_inc(s["var_done"], 1)
                dve.wait_ge(s["std_done"], k + 1)
                nc.vector.reciprocal(rstd[:], rstd[:]).then_inc(s["rstd_done"], 1)
                dve.wait_ge(s["rstd_done"], k + 1)
                for b in range(B):
                    y = y_ln0 if k == 0 else y_ln
                    nc.vector.tensor_scalar(y[:, b, :], x_res[:, b, :], mean_var[:, b, 0:1], rstd[:, b:b + 1],
                                            ALU.subtract, ALU.mult).then_inc(s["ln_done"], 1)

            dve.wait_ge(s["wkv_hi"], 1)
            tt(w_lo[:, 0], wk_raw, w_hi[:, 0], ALU.subtract).then_inc(s["wkv_lo"], 1)
            for c in range(C):
                dve.wait_ge(s["ctx_hi"], c + 1)
                tt(x_lo[:, c, :], raw[:, c, :], x_hi[:, c, :], ALU.subtract).then_inc(s["ctx_lo"], 1)
            dve.wait_ge(s["wkv_hi"], 2)
            tt(w_lo[:, 1], wv_raw, w_hi[:, 1], ALU.subtract).then_inc(s["wkv_lo"], 1)
            dve.wait_ge(s["x_in"], 16)
            layer_norm(0, lambda b: None)
            dve.wait_ge(s["qzero"], 1)
            dve.wait_ge(s["cols_in"], 16)
            for hg in range(C):
                dve.wait_ge(s["q_psum"], hg + 1)
                for j in range(J):
                    rows = slice(j * HD, (j + 1) * HD)
                    nc.vector.tensor_scalar(blocks[rows, hg::C, j, :],
                                            ps[rows, 4 + hg, :].rearrange("p (b q) -> p b q", b=B),
                                            cols[rows, 0, hg:hg + 1], SCALE, ALU.add, ALU.mult).then_inc(s["q_evac"], 1)
            dve.wait_ge(s["rel_in"], 32)
            tt(eq_rel, eq_rel, ek_rel, ALU.mult).then_inc(s["pos_mul"], 1)
            dve.wait_ge(s["pos_mul"], 1)
            nc.vector.tensor_reduce(pos[:], eq_rel, AX.X, ALU.add).then_inc(s["pos_done"], 1)
            dve.wait_ge(s["small_in"], 48)
            nc.vector.scalar_tensor_tensor(soft[:, 0], temp[:], -1.0, temp[:], ALU.mult, ALU.min).then_inc(s["soft_a"], 1)

            def over_heads(t):
                return t[:, :].rearrange("p (o q) -> p o q", o=1).broadcast_to([P, H, P])

            def maxima(t, p):
                for b in range(B):
                    dve.wait_ge(s["s_evac"], 16 * t + 4 * b + 4)
                    nc.vector.tensor_reduce(m_part[:, b, :], s_buf[:, p, b * H:(b + 1) * H, :].rearrange("p h q -> p q h"),
                                            AX.X, ALU.max).then_inc(s["max_done"], 1)
                dve.wait_ge(s["max_done"], 4 * t + 4)
                nc.vector.tensor_reduce(m_all[:], m_part[:, :, :].rearrange("p b q -> p q b"), AX.X,
                                        ALU.max).then_inc(s["m_ready"], 1)

            def softmax(t, p):
                dve.wait_ge(s["m_ready"], t + 1)
                for b in range(B):
                    part = s_buf[:, p, b * H:(b + 1) * H, :]
                    tt(part, part, over_heads(m_all), ALU.subtract).then_inc(s["sub_done"], 1)
                for b in range(2):
                    dve.wait_ge(s["exp_done"], 4 * t + b + 1)
                    nc.vector.tensor_reduce(z_part[:, b, :], s_buf[:, p, b * H:(b + 1) * H, :].rearrange("p h q -> p q h"),
                                            AX.X, ALU.add).then_inc(s["sum_dve"], 1)
                dve.wait_ge(s["sum_dve"], 2 * t + 2)
                tt(z_part[:, 0], z_part[:, 0], z_part[:, 1], ALU.add).then_inc(s["z_done"], 1)
                dve.wait_ge(s["z_done"], 2 * t + 1)
                dve.wait_ge(s["zpool"], t + 1)
                tt(z_part[:, 0], z_part[:, 0], z_part[:, 2], ALU.add).then_inc(s["z_done"], 1)
                dve.wait_ge(s["z_done"], 2 * t + 2)
                if not (isinstance(t, int) and t == 0):
                    dve.wait_ge(s["attn_pool"], t)
                nc.vector.reciprocal(r_all[:], z_part[:, 0]).then_inc(s["r_ready"], 1)
                dve.wait_ge(s["r_ready"], t + 1)
                for b in range(3):
                    part = s_buf[:, p, b * H:(b + 1) * H, :]
                    tt(part, part, over_heads(r_all), ALU.mult).then_inc(s["attn_dve"], 1)

            def first():
                maxima(0, 0)

            def stage(t, p):
                softmax(t, p)
                maxima(t + 1, 1 - p)

            def last():
                softmax(T - 1, 1)

            schedule(dve, first, stage, last)

            def split_lo(c, bank, n):
                dve.wait_ge(s["x_hi_done"], C * n + c + 1)
                tt(x_lo[:, c, :], ps[:, bank, :], x_hi[:, c, :], ALU.subtract).then_inc(s["x_lo_done"], 1)

            for b in range(B):
                split_lo(b, 4 + b, 1)
            dve.wait_ge(s["xb_done"], 1)
            for b in range(B):
                dve.wait_ge(s["wo_psum"], b + 1)
                tt(x_res[:, b, :], ps[:, b, :], x_res[:, b, :], ALU.add).then_inc(s["x1_done"], 1)
            layer_norm(1, lambda b: dve.wait_ge(s["x1_done"], b + 1))
            dve.wait_ge(s["soft_c"], 1)
            nc.vector.scalar_tensor_tensor(soft[:, 0], temp[:], 0.0, soft[:, 2], ALU.max, ALU.add).then_inc(s["soft_d"], 1)
            for c in range(C):
                split_lo(c, 4 + c, 2)
            for hg in range(C):
                dve.wait_ge(s["qh"], hg + 1)
                tt(q_rest[:, hg, :], k_t[:, hg, :], q_parts[:, 0, hg, :], ALU.subtract).then_inc(s["qr"], 1)
            for hg in range(C):
                dve.wait_ge(s["qm"], hg + 1)
                tt(q_parts[:, 2, hg, :], q_rest[:, hg, :], q_parts[:, 1, hg, :], ALU.subtract).then_inc(s["ql"], 1)
            kf = v_buf[:, 0]
            for hg in range(C):
                dve.wait_ge(s["kf_evac"], hg + 1)
                for j in range(J):
                    rows = slice(j * HD, (j + 1) * HD)
                    nc.vector.tensor_copy(blocks[rows, hg::C, j, :],
                                          kf[rows, hg, :].rearrange("p (b q) -> p b q", b=B)).then_inc(s["k2_blocks"], 1)
                dve.wait_ge(s["kh"], hg + 1)
                dve.wait_ge(s["k2_blocks"], 4 * hg + 4)
                tt(kf[:, hg, :], kf[:, hg, :], k_parts[:, 0, hg, :], ALU.subtract).then_inc(s["kr"], 1)
            for hg in range(C):
                dve.wait_ge(s["km"], hg + 1)
                tt(k_parts[:, 2, hg, :], kf[:, hg, :], k_parts[:, 1, hg, :], ALU.subtract).then_inc(s["kl"], 1)
            dve.wait_ge(s["pos_done"], 1)
            dve.wait_ge(s["attn_dve"], 3 * T)
            for n in range(16):
                dve.wait_ge(s["rq_psum"], n + 1)
                pm = pos[:, 8 * n:8 * n + 8].rearrange("p (m o) -> p m o", o=1).broadcast_to([P, 8, B * H])
                tt(s_buf[:, 0, :, 8 * n:8 * n + 8].rearrange("p n m -> p m n"),
                   ps[:, n % 8, :].rearrange("p (m n) -> p m n", m=8), pm, ALU.add).then_inc(s["rq_evac"], 1)
            dve.wait_ge(s["rq_evac"], 16)

            def keys(t, b):
                return t[:, b * H:(b + 1) * H].rearrange("p (h o) -> p h o", o=1).broadcast_to([P, H, P])

            lg4 = s_buf[:, 0].rearrange("p (j c b) q -> p j c b q", j=J, c=C)
            for b in range(B):
                for hg in range(C):
                    g = b * C + hg
                    dve.wait_ge(s["lg_psum"], g + 1)
                    part = lg4[:, :, hg, b, :]
                    tt(part, ps[:, g % 8, :].rearrange("p (j m) -> p j m", j=J), part, ALU.add).then_inc(s["lg_done"], 1)
                dve.wait_ge(s["lg_done"], C * (b + 1))
                part = lg[:, :, b, :]
                nc.vector.tensor_reduce(rmax[:, b * H:(b + 1) * H], part, AX.X, ALU.max).then_inc(s["max2"], 1)
                if b < 2:
                    dve.wait_ge(s["max2"], b + 1)
                    tt(part, part, keys(rmax, b), ALU.subtract).then_inc(s["sub2_dve"], 1)
            for b in range(B):
                dve.wait_ge(s["exp2"], b + 1)
                nc.vector.tensor_reduce(rsum[:, b * H:(b + 1) * H], lg[:, :, b, :], AX.X, ALU.add).then_inc(s["sum2"], 1)
            dve.wait_ge(s["sum2"], B)
            nc.vector.reciprocal(rinv[:], rsum[:]).then_inc(s["rinv2"], 1)
            for g in range(1, G, 2):
                dve.wait_ge(s["at_psum"], g + 1)
                nc.vector.tensor_copy(probs_t[:, g, :, :], ps[:, g % 4, :].rearrange("p (j q) -> p j q", j=J)).then_inc(s["at_dve"], 1)
            dve.wait_ge(s["ot2_evac"], B)
            dve.wait_ge(s["ev2"], 4)
            ev_part = ps[:, 0:4, :].rearrange("p a n -> p (a n)").rearrange("p (q g j) -> p g q j", g=G, j=J)
            out_t = k_t[:, :, :].rearrange("p b (c q i) -> p (b c) q i", c=C, i=4)
            for i in range(4):
                for j in range(J):
                    dst = out_t[j * HD:(j + 1) * HD, :, :, i]
                    tt(dst, ev_part[i * HD:(i + 1) * HD, :, :, j], dst, ALU.add).then_inc(s["ot2_done"], 1)
            dve.wait_ge(s["rinv2"], 1)
            for b in range(B):
                dve.wait_ge(s["back_psum"], b + 1)
                r = rinv[:, b * H:(b + 1) * H].rearrange("p (j c o) -> p c j o", j=J, o=1).broadcast_to([P, C, J, HD])
                tt(v_buf[:, 0, b, :].rearrange("p (c j d) -> p c j d", c=C, j=J),
                   ps[:, 4 + b, :].rearrange("p (c j d) -> p c j d", c=C, j=J), r, ALU.mult).then_inc(s["back_mul"], 1)
            for b in range(B):
                dve.wait_ge(s["back_mul"], b + 1)
                tt(x_res[:, b, :], x_res[:, b, :], v_buf[:, 0, b, :], ALU.add).then_inc(s["x2_done"], 1)
            layer_norm(2, lambda b: dve.wait_ge(s["x2_done"], b + 1))
            for c in range(C):
                split_lo(c, c, 3)

            dve.wait_ge(s["b3_in"], 16)
            q3 = s_buf[:, 1, 0:16, :].rearrange("p (b a) n -> p b (a n)", b=B)
            for b in range(B):
                dve.wait_ge(s["q3_psum"], b + 1)
                tt(q3[:, b, :], ps[:, 4 + b, :], bias3[:, 0, :], ALU.add).then_inc(s["q3_bias"], 1)
            for hg in range(C):
                dve.wait_ge(s["k3_psum"], hg + 1)
                for j in range(J):
                    rows = slice(j * HD, (j + 1) * HD)
                    nc.vector.tensor_scalar(blocks[rows, hg::C, j, :],
                                            ps[rows, hg, :].rearrange("p (b q) -> p b q", b=B),
                                            cols[rows, 2, hg:hg + 1], None, ALU.add).then_inc(s["k3_blocks"], 1)
            dve.wait_ge(s["q3_sq"], 1)
            sq = s_buf[:, 1, 16:32, :].rearrange("p a n -> p (a n)").rearrange("p (n d) -> p n d", d=HD)
            nc.vector.tensor_reduce(rsum[:], sq, AX.X, ALU.add).then_inc(s["q3_ss"], 1)
            for b in range(B):
                dve.wait_ge(s["v3_psum"], b + 1)
                tt(v_buf[:, 1, b, :], ps[:, 4 + b, :], bias3[:, 2, :], ALU.add).then_inc(s["v3_done"], 1)
            dve.wait_ge(s["q3_rt"], 1)
            nc.vector.reciprocal(rinv[:], rsum[:]).then_inc(s["q3_rn"], 1)
            dve.wait_ge(s["q3_rn"], 1)
            q3h = s_buf[:, 1, 0:16, :].rearrange("p a n -> p (a n)").rearrange("p (n d) -> p n d", d=HD)
            tt(q3h, q3h, rinv[:, :].rearrange("p (n o) -> p n o", o=1).broadcast_to([P, B * H, HD]),
               ALU.mult).then_inc(s["q3_a"], 1)
            dve.wait_ge(s["q3_a"], 1)
            tt(q3, q3, bias3[:, 1:2, :].broadcast_to([P, B, D]), ALU.add).then_inc(s["q3_b"], 1)
            dve.wait_ge(s["q3_b"], 1)
            dve.wait_ge(s["soft_d"], 1)
            for b in range(B):
                dst = q3h[:, b * H:(b + 1) * H, :]
                last = tt(dst, dst, soft[:, 0, :].rearrange("p (h o) -> p h o", o=1).broadcast_to([P, H, HD]), ALU.mult)
            last.then_inc(s["q3_done"], 1)
            for b in range(B):
                dve.wait_ge(s["lg3_psum"], C * (b + 1))
                bank = 4 * (b % 2)
                part = ps[:, bank:bank + 4, :].rearrange("p a n -> p (a n)").rearrange("p (h m) -> p h m", m=P)
                nc.vector.tensor_reduce(rmax[:, b * H:(b + 1) * H], part, AX.X, ALU.max).then_inc(s["max3"], 1)
                dve.wait_ge(s["max3"], b + 1)
                tt(s_buf[:, 0, b * H:(b + 1) * H, :], part, keys(rmax, b), ALU.subtract).then_inc(s["sub3"], 1)
            for b in (2, 3, 0, 1):
                n = (2, 3, 0, 1).index(b)
                dve.wait_ge(s["exp3"], b + 1)
                nc.vector.tensor_reduce(rsum[:, b * H:(b + 1) * H], s_buf[:, 0, b * H:(b + 1) * H, :], AX.X,
                                        ALU.add).then_inc(s["sum3"], 1)
                dve.wait_ge(s["sum3"], n + 1)
                nc.vector.reciprocal(rinv[:, b * H:(b + 1) * H], rsum[:, b * H:(b + 1) * H]).then_inc(s["rinv3"], 1)
            for b in range(2):
                dve.wait_ge(s["rinv3"], 3 + b)
                part = s_buf[:, 0, b * H:(b + 1) * H, :]
                tt(part, part, keys(rinv, b), ALU.mult).then_inc(s["nrm3_dve"], 1)
            for g in range(1, G, 2):
                dve.wait_ge(s["at3_psum"], g + 1)
                nc.vector.tensor_copy(probs_t[:, g, :, :], ps[:, g % 4, :].rearrange("p (j q) -> p j q", j=J)).then_inc(s["at3_dve"], 1)
            for b in range(B):
                dve.wait_ge(s["ot3_hi"], b + 1)
                tt(x_lo[:, b, :], k_t[:, b, :], x_hi[:, b, :], ALU.subtract).then_inc(s["ot3_lo"], 1)
            for b in range(B):
                dve.wait_ge(s["g_psum"], b + 1)
                tt(gate[:, b, :], ps[:, 4 + b, 0:NG], b_gate[:], ALU.add).then_inc(s["g_bias"], 1)
            dve.wait_ge(s["g_bias"], B)
            routed, shared = gate[:, :, 0:NR], gate[:, :, NR:NG]
            nc.vector.tensor_reduce(gtmp[:, :, 0], routed, AX.X, ALU.max).then_inc(s["g_max"], 1)
            nc.vector.tensor_reduce(gtmp[:, :, 1], shared, AX.X, ALU.max).then_inc(s["g_max"], 1)
            dve.wait_ge(s["g_max"], 2)
            tt(routed, routed, gtmp[:, :, 0:1].broadcast_to([P, B, NR]), ALU.subtract).then_inc(s["g_sub"], 1)
            tt(shared, shared, gtmp[:, :, 1:2].broadcast_to([P, B, 2]), ALU.subtract).then_inc(s["g_sub"], 1)
            dve.wait_ge(s["g_exp"], 1)
            for b in range(B):
                nc.vector.max(top8[:, b, :], gate[:, b, 0:NR]).then_inc(s["g_top"], 1)
            nc.vector.tensor_reduce(gtmp[:, :, 2], routed, AX.X, ALU.add).then_inc(s["g_c1"], 1)
            nc.vector.tensor_reduce(gtmp[:, :, 3], shared, AX.X, ALU.add).then_inc(s["g_c1"], 1)
            dve.wait_ge(s["g_top"], B)
            nc.vector.tensor_reduce(gtmp[:, :, 4], top8[:, :, 0:3], AX.X, ALU.add).then_inc(s["g_c1"], 1)
            dve.wait_ge(s["g_c1"], 3)
            nc.vector.reciprocal(gtmp[:, :, 2:4], gtmp[:, :, 2:4]).then_inc(s["g_c2"], 1)
            dve.wait_ge(s["g_c2"], 1)
            tt(shared, shared, gtmp[:, :, 3:4].broadcast_to([P, B, 2]), ALU.mult).then_inc(s["g_c3"], 1)
            nc.vector.scalar_tensor_tensor(gtmp[:, :, 4], gtmp[:, :, 4], 3.0, gtmp[:, :, 2], ALU.mult,
                                           ALU.mult).then_inc(s["g_c3"], 1)
            dve.wait_ge(s["g_c3"], 2)
            tt(gtmp[:, :, 5], gate[:, :, NR], gate[:, :, NR + 1], ALU.add).then_inc(s["g_c4"], 1)
            nc.vector.scalar_tensor_tensor(gtmp[:, :, 6], gate[:, :, NR + 1], 2.0, gtmp[:, :, 4], ALU.mult,
                                           ALU.mult).then_inc(s["g_c4"], 1)
            dve.wait_ge(s["g_c4"], 2)
            nc.vector.scalar_tensor_tensor(gtmp[:, :, 7], gate[:, :, NR], 2.0, gtmp[:, :, 5], ALU.mult,
                                           ALU.mult).then_inc(s["g_c5"], 1)
            dve.wait_ge(s["g_c5"], 1)
            tt(rstd[:], gtmp[:, :, 6], gtmp[:, :, 7], ALU.add).then_inc(s["g_c6"], 1)
            dve.wait_ge(s["g_c6"], 1)
            dve.wait_ge(s["xp_done"], 1)
            for b in range(B):
                dve.wait_ge(s["y_psum"], b + 1)
                nc.vector.scalar_tensor_tensor(x_res[:, b, :], ps[:, b, :], rstd[:, b:b + 1], x_res[:, b, :],
                                               ALU.mult, ALU.add).then_inc(s["fin_done"], 1)


def kernel(**inputs):
    import concourse.bacc as bacc
    from concourse.bass_utils import run_bass_kernel_spmd

    f = {k: np.asarray(v) for k, v in inputs.items()}

    def chunks(w):
        return w.reshape(C, P, -1).transpose(1, 0, 2)

    rel = np.clip(np.arange(P)[:, None] - np.arange(P)[None, :], -64, 64) + 64
    span = np.arange(2 * P - 1)
    arrays = {
        "x": f["x"],
        "ctxT": f["ctx_1024"].reshape(B, T, P, C, P).transpose(1, 4, 3, 0, 2).reshape(T, P, C, D),
        "Wq1": chunks(f["L0_xattn_Wq"]), "Wk1": chunks(f["L0_xattn_Wk"]), "Wv1": chunks(f["L0_xattn_Wv"]),
        "Wo1": chunks(f["L0_xattn_Wo"]), "bv1": f["L0_xattn_bv"], "bo1": f["L0_xattn_bo"],
        "cols": np.stack([f["L0_xattn_bq"], f["L0_xattn_bk"], f["L0_ffn_bk"]]).reshape(3, C, P).transpose(2, 0, 1),
        "Wq2": chunks(f["L0_attn_Wq"]), "Wk2": chunks(f["L0_attn_Wk"]), "Wv2": chunks(f["L0_attn_Wv"]),
        "EqRel": f["L0_attn_Eq"][rel], "EkRel": f["L0_attn_Ek"][rel],
        "EvRel": f["L0_attn_Ev"][rel.T],
        "EkTab": np.tile(f["L0_attn_Ek"][np.clip(127 - span, -64, 64) + 64].T, (3, 1)),
        "EqTab": np.tile(f["L0_attn_Eq"][np.clip(span - 127, -64, 64) + 64].T, (3, 1)),
        "Wq3": chunks(f["L0_ffn_Wq"].T), "Wk3": chunks(f["L0_ffn_Wk"].T), "Wv3": chunks(f["L0_ffn_Wv"].T),
        "Wp3": chunks(f["L0_ffn_Wp"].T),
        "Wg": chunks(np.concatenate([f["L0_ffn_Wr"], f["L0_ffn_Ws"]]).T),
        "bg": np.concatenate([f["L0_ffn_br"], f["L0_ffn_bs"]]),
        "temp": f["L0_ffn_temperature"].reshape(H),
        "bias3": np.stack([f["L0_ffn_bq"], f["L0_ffn_query_embedding"].reshape(D), f["L0_ffn_bv"], f["L0_ffn_bp"]]),
    }
    arrays = {k: np.ascontiguousarray(v) for k, v in arrays.items()}
    nc = bacc.Bacc("TRN2", target_bir_lowering=False, num_devices=1)
    aps = {k: nc.dram_tensor("in_" + k, v.shape, mybir.dt.from_np(v.dtype), kind="ExternalInput").ap()
           for k, v in arrays.items()}
    out = nc.dram_tensor("out", (B, P, D), F32, kind="ExternalOutput").ap()
    program(nc, aps, out)
    r = run_bass_kernel_spmd(nc, [{"in_" + k: v for k, v in arrays.items()}], core_ids=[0])
    return r.results[0]["out"]
```

```python
from contextlib import ExitStack

import concourse.bass as bass
import numpy as np
from concourse import mybir

F32 = mybir.dt.float32
F32R = mybir.dt.float32r
BF16 = mybir.dt.bfloat16
ACT = mybir.ActivationFunctionType
ALU = mybir.AluOpType
AX = mybir.AxisListType

P = 128
B = 4
D = 512
C = D // P
H = 16
HD = D // H
J = P // HD
G = B * C
SK = 2048
T = SK // P
NR = 15
NG = NR + 2
EPS = 1e-5
SCALE = float(HD) ** -0.5


def program(nc, a, out):
    with ExitStack() as ctx:
        def sb(name, shape, dt=F32):
            return ctx.enter_context(nc.sbuf_tensor(name, shape, dt))

        def sem(name):
            return ctx.enter_context(nc.semaphore(name))

        x_res = sb("x_res", [P, B, D])
        blocks = sb("blocks", [P, G, J, P])
        s_buf = sb("s_buf", [P, 2, B * H, P])
        raw = sb("raw", [P, C, D])
        x_hi = sb("x_hi", [P, C, D], F32R)
        x_lo = sb("x_lo", [P, C, D], F32R)
        w_hi = sb("w_hi", [P, 2, C, D], F32R)
        w_lo = sb("w_lo", [P, 2, C, D], F32R)
        k_t = sb("k_t", [P, C, D])
        v_buf = sb("v_buf", [P, 2, B, D])
        extra = sb("extra", [P, 4096])
        pool_tmp = extra[:, 0:1024]
        bv_all = extra[:, 2048:2560]
        m_part = extra[:, 2560:3072].rearrange("p (b q) -> p b q", b=B)
        bo_all = extra[:, 3072:3584]
        z_part = extra[:, 1024:1536].rearrange("p (n q) -> p n q", n=4)
        ev_rel = extra[:, :].rearrange("p (l d) -> p l d", d=HD)
        bias3 = extra[:, 0:2048].rearrange("p (n e) -> p n e", n=4)
        z_all = extra[:, 1536:1664]
        ident = sb("ident", [P, P])
        m_all = sb("m_all", [P, P])
        r_all = sb("r_all", [P, P])
        ek_parts = sb("ek_parts", [3 * HD, 3, 2 * P], BF16)
        eq_parts = sb("eq_parts", [3 * HD, 3, 2 * P], BF16)
        pos = sb("pos", [P, P])
        cols = sb("cols", [P, 3, C])
        bq_scaled = sb("bq_scaled", [P, C])
        stats = sb("stats", [P, B, 6])
        mean_var = sb("mean_var", [P, B, 2])
        rstd = sb("rstd", [P, B])
        temp = sb("temp", [P, H])
        soft = sb("soft", [P, 3, H])
        rmax = sb("rmax", [P, B * H])
        rsum = sb("rsum", [P, B * H])
        rinv = sb("rinv", [P, B * H])
        neg_max = sb("neg_max", [P, B * H])
        w_gate = sb("w_gate", [P, C, NG])
        b_gate = sb("b_gate", [P, NG])
        gate = sb("gate", [P, B, NG])
        gtmp = sb("gtmp", [P, B, 8])
        top8 = sb("top8", [P, B, 8])
        ps = ctx.enter_context(nc.psum_tensor("ps", [P, 8, 512], F32))

        def half(n, lo, hi):
            return s_buf[:, n, lo:hi, :].rearrange("p (c a) q -> p c (a q)", a=4)

        def as_bf16(t, n):
            return t.rearrange("p a q -> p (a q)").bitcast(BF16)[:, 0:n]

        RING = 6
        groups = s_buf[:, :, :, :].rearrange("p n h q -> p (n h) q")

        EXP_ORDER = (1, 0, 2, 3)

        def scores(k, b):
            n = (B * k + b) % RING
            return groups[:, n * H:(n + 1) * H, :]

        k1_pack = as_bf16(groups[:, RING * H:, :], 8192)
        q1_packs = as_bf16(blocks[:, :, :, :].rearrange("p g j q -> p (g j) q"), 16384)
        q1_pack_a, q1_pack_b = q1_packs[:, 0:8192], q1_packs[0:3 * HD, 8192:16384]
        k1_high = extra[:, 3072:4096].bitcast(BF16).rearrange("p (c n) -> p c n", c=C)
        k1_rest = as_bf16(x_res, 4096).rearrange("p (r c n) -> p r c n", r=2, c=C)
        k1_parts = (k1_high, k1_rest[:, 0], k1_rest[:, 1])
        q1_float = v_buf[:, 1]
        q1_parts_all = as_bf16(s_buf[:, 0, 32:56, :], 3 * 2048).rearrange("p (r c n) -> p r c n", r=3, c=C)
        q1_parts = tuple(q1_parts_all[:, r] for r in range(3))

        y_ln0, y_ln = v_buf[:, 1], v_buf[:, 0]
        x_t0, wq_raw, wk_raw, wv_raw = (half(0, 16 * n, 16 * n + 16) for n in range(4))
        tab_raw = k_t[0:3 * HD, 0:2, 0:2 * P]
        eq_rel = s_buf[:, 1, 0:32, :].rearrange("p h (m d) -> p (h m) d", d=HD)
        ek_rel = s_buf[:, 1, 32:64, :].rearrange("p h (m d) -> p (h m) d", d=HD)
        q_parts = as_bf16(s_buf[:, 1, 0:24, :], 3 * 2048).rearrange("p (r c n) -> p r c n", r=3, c=C)
        q_rest = half(1, 32, 48)
        k_parts = as_bf16(s_buf[:, 0, 32:56, :], 3 * 2048).rearrange("p (r c n) -> p r c n", r=3, c=C)
        q_pack = as_bf16(s_buf[:, 0, 0:32, :], 8192)
        k_pack = extra[:, :].bitcast(BF16)
        ev_half = v_buf[:, 1, 0:2, :].rearrange("p b n -> p (b n)").rearrange("p (g q i) -> p g q i", g=G, i=2)
        probs_t = s_buf[:, 1].rearrange("p (g j) q -> p g j q", j=J)
        lg = s_buf[:, 0].rearrange("p (n b) q -> p n b q", b=B)

        SPLIT = 2

        def exp2_count(b):
            return H * min(b + 1, SPLIT) + max(b + 1 - SPLIT, 0)

        names = """x_in wq_in wk_in wv_in cols_in bv_in bo_in tab_in ctx_in ctx_hi ctx_lo wkv_hi wkv_lo wraw_in wsplit_hi wsplit_lo
            tab_steps x_hi_done x_lo_done rel_in small_in
            ident_done qzero stats_done mv_done var_done std_done rstd_done ln_done tr_done q_psum bq_done xb_done
            pos_mul pos_done
            q1_float q1_high q1_rest q1_mid q1_low q1_high_in q1_mid_in q1_pack_in k1_high_in k1_high k1_rest k1_mid k1_low k1_pack_in
            kv_psum kv_evac v_ready s_psum s_evac max_done m_ready sub_done sub_pool exp_done
            sum_dve zadd zpool z_done r_ready attn_dve attn_pool av_done
            wo_psum x1_done
            ev_in qpack_in kpack_in qh qr qm ql kf_evac kh kr km kl
            q2_psum q2_evac k2_psum k2_blocks v2_psum v2_evac
            rk_psum rk_evac rq_psum rq_evac lg_psum lg_done max2 neg2 sub2 exp2 sum2 rinv2
            at_psum at_done av2 ev2 ev_copied ot2_evac ot2_done back_psum back_mul x2_done
            soft_a soft_b soft_c soft_d
            b3_in xp_done
            q3_psum q3_bias q3_sq q3_ss q3_rt q3_rn q3_rsp qe_done q3_a q3_done q3t_psum q3t_evac k3_psum k3_blocks k3_blocks_act v3_psum v3_done
            lg3_psum max3 sub3 exp3 sum3 rinv3 rexp3 rb_psum ot3_done at3_psum at3_done av3 ot3_evac ot3_hi ot3_lo
            g_psum g_bias g_max g_sub g_exp g_top g_steps y_psum fin_done out_done""".split()
        s = {n: sem(n) for n in names}

        block = ctx.enter_context(nc.Block())

        assert (T - 4) % 6 == 0 and SPLIT <= B

        def schedule(eng, first, stage, last):
            first()
            stage(0, 0)
            with eng.Fori(0, (T - 4) // 6) as i:
                for u in range(1, 7):
                    stage(6 * i + u, u % 6)
            stage(T - 3, (T - 3) % 6)
            stage(T - 2, (T - 2) % 6)
            last()

        WEIGHTS = [("Wo1", "kv_psum", 8 * T), ("Wq2", "kv_psum", 8 * T), ("Wk2", "wo_psum", B), ("Wv2", "q2_psum", C),
                   ("Wq3", "k2_psum", C), ("Wk3", "v2_psum", B), ("Wv3", "q3_psum", B), ("Wp3", "k3_psum", C)]

        @block.sync
        def _(sp):
            def load(dst, src, name):
                sp.dma_start(dst, src).then_inc(s[name], 16)

            x_rows = a["x"].rearrange("b q e -> q b e")
            load(x_res[:], x_rows, "x_in")
            load(wq_raw, a["Wq1"], "wq_in")
            load(cols[:], a["cols"], "cols_in")
            load(wk_raw, a["Wk1"], "wk_in")
            load(raw[:], a["ctxT"][0], "ctx_in")
            load(tab_raw[:, 0, 0:2 * P - 1], a["EkTab"], "tab_in")
            load(tab_raw[:, 1, 0:2 * P - 1], a["EqTab"], "tab_in")
            load(wv_raw, a["Wv1"], "wv_in")
            load(bv_all, a["bv1"].partition_broadcast(P), "bv_in")
            load(eq_rel, a["EqRel"], "rel_in")
            load(ek_rel, a["EkRel"], "rel_in")

            def ctx_load(t):
                sp.wait_ge(s["ctx_hi"], C * t)
                sp.wait_ge(s["ctx_lo"], C * t)
                load(raw[:], a["ctxT"][t], "ctx_in")

            ctx_load(1)
            load(temp[:], a["temp"].partition_broadcast(P), "small_in")
            load(w_gate[:], a["Wg"], "small_in")
            load(b_gate[:], a["bg"].partition_broadcast(P), "small_in")

            def group(dst, r, part, landed):
                for j in range(J):
                    load(dst[r * HD:(r + 1) * HD, j * 2048:(j + 1) * 2048],
                         part[j * HD:(j + 1) * HD].rearrange("p c n -> p (c n)"), landed)

            def again(dst, r, src, q, landed):
                load(dst[r * HD:(r + 1) * HD, :], src[q * HD:(q + 1) * HD, :], landed)

            def k_pack1(n):
                if not (isinstance(n, int) and n == 1):
                    sp.wait_ge(s["s_psum"], 16 * n - 16)
                sp.wait_ge(s["k1_high"], C * n)
                group(k1_pack, 0, k1_parts[0], "k1_high_in")
                sp.wait_ge(s["k1_mid"], C * n)
                group(k1_pack, 1, k1_parts[1], "k1_pack_in")
                sp.wait_ge(s["k1_high_in"], 64 * n)
                again(k1_pack, 3, k1_pack, 0, "k1_pack_in")
                sp.wait_ge(s["k1_low"], C * n)
                group(k1_pack, 2, k1_parts[2], "k1_pack_in")

            sp.wait_ge(s["q1_high"], C)
            group(q1_pack_a, 0, q1_parts[0], "q1_high_in")
            sp.wait_ge(s["q1_mid"], C)
            group(q1_pack_a, 3, q1_parts[1], "q1_mid_in")
            sp.wait_ge(s["q1_high_in"], 64)
            again(q1_pack_a, 1, q1_pack_a, 0, "q1_pack_in")
            again(q1_pack_a, 2, q1_pack_a, 0, "q1_pack_in")
            sp.wait_ge(s["q1_low"], C)
            group(q1_pack_b, 0, q1_parts[2], "q1_pack_in")
            sp.wait_ge(s["q1_mid_in"], 64)
            again(q1_pack_b, 1, q1_pack_a, 3, "q1_pack_in")
            again(q1_pack_b, 2, q1_pack_a, 3, "q1_pack_in")
            sp.wait_ge(s["pos_mul"], 1)
            k_pack1(1)
            with sp.Fori(2, T) as t:
                ctx_load(t)
                k_pack1(t)
            k_pack1(T)
            sp.wait_ge(s["k1_pack_in"], 144 * T)
            load(x_res[:], x_rows, "x_in")
            load(bo_all, a["bo1"].partition_broadcast(P), "bo_in")

            def weight_load(n):
                if n == 0:
                    sp.wait_ge(s["ctx_hi"], C * T)
                    sp.wait_ge(s["ctx_lo"], C * T)
                else:
                    sp.wait_ge(s["wsplit_lo"], n)
                load(raw[:], a[WEIGHTS[n][0]], "wraw_in")

            def pack(dst, parts, done, landed):
                sp.wait_ge(s[done], C)
                for r in range(3):
                    for j in range(J):
                        load(dst[r * HD:(r + 1) * HD, j * 2048:(j + 1) * 2048],
                             parts[j * HD:(j + 1) * HD, r].rearrange("p c n -> p (c n)"), landed)

            for n in range(4):
                weight_load(n)
            pack(q_pack, q_parts, "ql", "qpack_in")
            weight_load(4)
            pack(k_pack, k_parts, "kl", "kpack_in")
            weight_load(5)
            sp.wait_ge(s["rq_psum"], 16)
            load(ev_rel, a["EvRel"], "ev_in")
            weight_load(6)
            sp.wait_ge(s["ev2"], 4)
            load(bias3, a["bias3"].rearrange("(o n) e -> o n e", o=1).broadcast_to([P, 4, D]), "b3_in")
            weight_load(7)
            for b in range(B):
                sp.wait_ge(s["fin_done"], b + 1)
                sp.dma_start(out[b], x_res[:, b, :]).then_inc(s["out_done"], 16)
            sp.wait_ge(s["out_done"], 16 * B)

        @block.tensor
        def _(pe):
            mm = nc.tensor.matmul

            PARTS = ((0, 0), (0, 1), (1, 0))
            x_parts, w_parts = (x_hi, x_lo), (w_hi, w_lo)

            def transposes(y, banks, k):
                for c in range(C):
                    for b in range(B):
                        if c == 0:
                            pe.wait_ge(s["ln_done"], B * k + b + 1)
                        last = nc.tensor.transpose(ps[:, banks + c, b * P:(b + 1) * P], y[:, b, c * P:(c + 1) * P], ident[:])
                    last.then_inc(s["tr_done"], 1)

            def proj_t(slot, bank, done, hg, low_ready=None):
                for n, (u, v) in enumerate(PARTS):
                    if n == 2 and low_ready is not None:
                        pe.wait_ge(s["ctx_lo"], low_ready)
                    for c in range(C):
                        last = mm(ps[:, bank, :], w_parts[v][:, slot, c, hg * P:(hg + 1) * P], x_parts[u][:, c, :],
                                  start=n + c == 0, stop=n == 2 and c == C - 1)
                last.then_inc(done, 1)

            def proj_n(slot, bank, done, b):
                for n, (u, v) in enumerate(PARTS):
                    for c in range(C):
                        last = mm(ps[:, bank, :], x_parts[u][:, c, b * P:(b + 1) * P], w_parts[v][:, slot, c, :],
                                  start=n + c == 0, stop=n == 2 and c == C - 1)
                last.then_inc(done, 1)

            def out_proj(slot, bank, done, b):
                for n, (u, v) in enumerate(PARTS):
                    for c in range(C):
                        last = mm(ps[:, bank, :], x_parts[u][:, b, c * P:(c + 1) * P], w_parts[v][:, slot, c, :],
                                  start=n + c == 0, stop=n == 2 and c == C - 1)
                last.then_inc(done, 1)

            def weight_ready(n):
                pe.wait_ge(s["wsplit_lo"], n + 1)

            def project(t, which):
                for n in which:
                    if n == 0:
                        pe.wait_ge(s["ctx_hi"], C * t + C)
                    if n >= 2 or not (isinstance(t, int) and t == 0):
                        pe.wait_ge(s["kv_evac"], 8 * t + n - 1)
                    if isinstance(t, int) and t == 0 and n % 4 == 0:
                        pe.wait_ge(s["wkv_lo"], 1 + n // 4)
                    if n < 4:
                        proj_t(0, n % 2, s["kv_psum"], n, low_ready=C * t + C if n == 0 else None)
                    else:
                        proj_n(1, n % 2, s["kv_psum"], n - 4)

            def score(t, b, chunks=range(C)):
                for hg in chunks:
                    g = b * C + hg
                    if g == 0:
                        pe.wait_ge(s["k1_pack_in"], 144 * t + 144)
                    if g >= 2 or not (isinstance(t, int) and t == 0):
                        pe.wait_ge(s["s_evac"], 16 * t + g - 1)
                    for j in range(J):
                        n = ((j * C + hg) * B + b) * P
                        dst = ps[:, 2 + g % 2, j * P:(j + 1) * P]
                        mm(dst, k1_pack[:, n:n + P], q1_pack_a[:, n:n + P], start=True, stop=False,
                           skip_group_check=True)
                        last = mm(dst, k1_pack[0:3 * HD, n:n + P], q1_pack_b[:, n:n + P], start=False, stop=True,
                                  skip_group_check=True)
                    last.then_inc(s["s_psum"], 1)

            def attend(t, k, b, first=False, final=False):
                pe.wait_ge(s["v_ready"], B * t + b + 1)
                if b < 3:
                    pe.wait_ge(s["attn_dve"], 3 * t + b + 1)
                else:
                    pe.wait_ge(s["attn_pool"], t + 1)
                for hg in range(C):
                    for j in range(J):
                        h = hg * J + j
                        last = mm(ps[j * HD:(j + 1) * HD, 4 + b, hg * P:(hg + 1) * P],
                                  v_buf[:, k % 2, b, h * HD:(h + 1) * HD], scores(k, b)[:, h, :],
                                  start=first and hg == 0, stop=final and hg == C - 1, skip_group_check=True)
                last.then_inc(s["av_done"], 1)

            def first():
                pe.wait_ge(s["ident_done"], 2)
                transposes(y_ln0, 4, 0)
                pe.wait_ge(s["wq_in"], 16)
                pe.wait_ge(s["x_hi_done"], C)
                for hg in range(C):
                    for c in range(C):
                        last = mm(ps[:, 4 + hg, :], wq_raw[:, c, hg * P:(hg + 1) * P], x_t0[:, c, :],
                                  start=c == 0, stop=c == C - 1)
                    last.then_inc(s["q_psum"], 1)
                project(0, range(8))
                pe.wait_ge(s["q1_pack_in"], 16 * 8)
                for n in range(4):
                    score(0, n // 2, (2 * (n % 2), 2 * (n % 2) + 1))
                    project(1, (n,))
                score(0, 2)
                score(0, 3)

            def stage(t, k):
                zero = isinstance(t, int) and t == 0
                more = not (isinstance(t, int) and t == T - 2)
                project(t + 1, range(4, 8))
                for n in range(4):
                    score(t + 1, n // 2, (2 * (n % 2), 2 * (n % 2) + 1))
                    if more:
                        project(t + 2, (n,))
                attend(t, k, 0, first=zero)
                score(t + 1, 2)
                attend(t, k, 1, first=zero)
                score(t + 1, 3)
                attend(t, k, 2, first=zero)
                attend(t, k, 3, first=zero)

            def last():
                for b in range(B):
                    attend(T - 1, (T - 1) % 6, b, final=True)

            schedule(pe, first, stage, last)

            weight_ready(0)
            for b in range(B):
                pe.wait_ge(s["x_lo_done"], b + 1)
                out_proj(0, b, s["wo_psum"], b)

            transposes(y_ln, 4, 1)
            weight_ready(1)
            pe.wait_ge(s["x_lo_done"], 2 * C)
            for hg in range(C):
                pe.wait_ge(s["x1_done"], hg + 1)
                proj_t(1, hg, s["q2_psum"], hg)
            weight_ready(2)
            for hg in range(C):
                proj_t(0, 4 + hg, s["k2_psum"], hg)
            weight_ready(3)
            for b in range(B):
                pe.wait_ge(s["q2_evac"], b + 1)
                proj_n(1, b, s["v2_psum"], b)

            def relative(parts, pack, psum_done, drained):
                for n in range(16):
                    drained(n)
                    for i in range(8):
                        r = 8 * n + i
                        rows = pack[0:3 * HD, :].rearrange("p (n q) -> p n q", q=P)[:, :, r]
                        for u in range(3):
                            last = mm(ps[:, n % 8, i * 64:(i + 1) * 64], parts[:, u, P - 1 - r:2 * P - 1 - r], rows,
                                      start=u == 0, stop=u == 2, skip_group_check=True)
                    last.then_inc(psum_done, 1)

            def rk_free(n):
                if n < 4:
                    pe.wait_ge(s["v2_evac"], n + 1)
                elif n < 8:
                    pe.wait_ge(s["kf_evac"], n - 3)
                else:
                    pe.wait_ge(s["rk_evac"], n - 7)

            def rq_free(n):
                if n < 8:
                    pe.wait_ge(s["rk_evac"], 8 + n + 1)
                else:
                    pe.wait_ge(s["rq_evac"], n - 7)

            pe.wait_ge(s["tab_steps"], 8)
            pe.wait_ge(s["qpack_in"], 16 * 12)
            relative(ek_parts, q_pack, s["rk_psum"], rk_free)
            pe.wait_ge(s["kpack_in"], 16 * 12)
            relative(eq_parts, k_pack, s["rq_psum"], rq_free)
            pe.wait_ge(s["k2_blocks"], 16)

            def logits(b):
                for hg in range(C):
                    g = b * C + hg
                    if g < 4:
                        pe.wait_ge(s["rq_evac"], 8 + g + 1)
                    else:
                        pe.wait_ge(s["lg_done"], g - 3)
                    for j in range(J):
                        mm(ps[:, hg, j * P:(j + 1) * P], s_buf[:, 1, (j * C + hg) * B + b, :], ident[:],
                           start=j == 0, stop=False, is_transpose=True, skip_group_check=True)
                    mm(ps[:, hg, :], k_t[:, hg, b * P:(b + 1) * P], blocks[:, g].rearrange("p j m -> p (j m)"),
                       start=False, stop=True, skip_group_check=True).then_inc(s["lg_psum"], 1)

            def attention_t(b):
                pe.wait_ge(s["exp2"], exp2_count(b))
                for hg in range(C):
                    g = b * C + hg
                    if g < 4:
                        pe.wait_ge(s["rq_evac"], 12 + g + 1)
                    else:
                        pe.wait_ge(s["at_done"], g - 3)
                    for j in range(J):
                        last = nc.tensor.transpose(ps[:, 4 + hg, j * P:(j + 1) * P], lg[:, j * C + hg, b, :], ident[:])
                    last.then_inc(s["at_psum"], 1)

            for b in range(B):
                logits(b)
            for b in range(B):
                attention_t(b)
            pe.wait_ge(s["lg_done"], G)
            for g in range(G):
                b, hg = divmod(g, C)
                pe.wait_ge(s["at_done"], g + 1)
                for j in range(J):
                    h = hg * J + j
                    last = mm(ps[j * HD:(j + 1) * HD, b, hg * P:(hg + 1) * P], v_buf[:, 1, b, h * HD:(h + 1) * HD],
                              probs_t[:, g, j, :], start=hg == 0, stop=hg == C - 1, skip_group_check=True)
                if hg == C - 1:
                    last.then_inc(s["av2"], 1)
            pe.wait_ge(s["ev_in"], 16)
            for bank in range(4):
                for n in range(32):
                    l, i = bank * 32 + n, n % 4
                    last = mm(ps[i * HD:(i + 1) * HD, 4 + bank, n // 4 * 64:(n // 4 + 1) * 64], ev_rel[:, l, :],
                              probs_t[:, :, :, l].rearrange("p g j -> p (g j)"), start=n < 4, stop=n >= 28,
                              skip_group_check=True)
                last.then_inc(s["ev2"], 1)
            pe.wait_ge(s["ot2_done"], 9)
            for b in range(B):
                for hg in range(C):
                    last = nc.tensor.transpose(ps[:, b, hg * P:(hg + 1) * P], k_t[:, b, hg * P:(hg + 1) * P], ident[:])
                last.then_inc(s["back_psum"], 1)

            transposes(y_ln, 4, 2)
            pe.wait_ge(s["x_lo_done"], 3 * C)
            weight_ready(4)
            for b in range(B):
                pe.wait_ge(s["back_mul"], b + 1)
                proj_n(0, b, s["q3_psum"], b)
            weight_ready(5)
            for hg in range(C):
                proj_t(1, 4 + hg, s["k3_psum"], hg)
            weight_ready(6)
            for b in range(B):
                pe.wait_ge(s["q3_bias"], b + 1)
                proj_n(0, b, s["v3_psum"], b)
            pe.wait_ge(s["k3_blocks"], 8)
            pe.wait_ge(s["k3_blocks_act"], 8)
            for b in range(B):
                pe.wait_ge(s["q3_done"], b + 1)
                for c in range(C):
                    last = nc.tensor.transpose(ps[:, 4 + c, b * P:(b + 1) * P], s_buf[:, 1, b * C + c, :], ident[:])
            last.then_inc(s["q3t_psum"], 1)

            def logits3(b):
                bank = 4 * (b % 2)
                if b == 0:
                    pe.wait_ge(s["v3_done"], B)
                    pe.wait_ge(s["q3t_evac"], C)
                if b >= 2:
                    pe.wait_ge(s["sub3"], b - 1)
                for hg in range(C):
                    mm(ps[:, bank + hg, :], s_buf[:, 1, 32 + 4 * hg + b, :],
                       blocks[:, b * C + hg].rearrange("p j m -> p (j m)"), start=True, stop=True).then_inc(s["lg3_psum"], 1)

            def attention3_t(b):
                pe.wait_ge(s["exp3"], b + 1)
                if b < 2:
                    pe.wait_ge(s["sub3"], b + 3)
                else:
                    pe.wait_ge(s["at3_done"], C * (b - 1))
                for hg in range(C):
                    g = b * C + hg
                    for j in range(J):
                        last = nc.tensor.transpose(ps[:, 4 * (b % 2) + hg, j * P:(j + 1) * P], s_buf[:, 0, g * J + j, :],
                                                   ident[:])
                    last.then_inc(s["at3_psum"], 1)

            for b in range(B):
                logits3(b)
            for b in range(B):
                attention3_t(b)
            for b in range(B):
                pe.wait_ge(s["at3_done"], G)
                for hg in range(C):
                    for j in range(J):
                        h = hg * J + j
                        last = mm(ps[j * HD:(j + 1) * HD, b, hg * P:(hg + 1) * P], v_buf[:, 1, b, h * HD:(h + 1) * HD],
                                  probs_t[:, b * C + hg, j, :], start=hg == 0, stop=hg == C - 1, skip_group_check=True)
                last.then_inc(s["av3"], 1)
            for b in range(B):
                pe.wait_ge(s["rexp3"], b + 1)
                for hg in range(C):
                    last = nc.tensor.transpose(ps[:, 4 + b, hg * P:(hg + 1) * P], v_buf[:, 0, b, hg * P:(hg + 1) * P],
                                               ident[:])
                last.then_inc(s["rb_psum"], 1)
            pe.wait_ge(s["small_in"], 48)
            for b in range(B):
                pe.wait_ge(s["ot3_done"], b + 1)
                for hg in range(C):
                    last = mm(ps[:, 4 + b, 0:NG], k_t[:, b, hg * P:(hg + 1) * P], w_gate[:, hg, :],
                              start=hg == 0, stop=hg == C - 1)
                last.then_inc(s["g_psum"], 1)
            weight_ready(7)
            for b in range(B):
                pe.wait_ge(s["ot3_lo"], b + 1)
                out_proj(1, b, s["y_psum"], b)

        @block.scalar
        def _(act):
            copy = nc.scalar.copy

            def ln_std(k):
                act.wait_ge(s["var_done"], k + 1)
                nc.scalar.activation(rstd[:], rstd[:], ACT.Sqrt).then_inc(s["std_done"], 1)

            def weight_hi(n):
                act.wait_ge(s["wraw_in"], 16 * (n + 1))
                act.wait_ge(s[WEIGHTS[n][1]], WEIGHTS[n][2])
                copy(w_hi[:, n % 2], raw[:]).then_inc(s["wsplit_hi"], 1)

            def ctx_split(t, b):
                if b == 0:
                    act.wait_ge(s["ctx_in"], 16 * t + 16)
                if not (isinstance(t, int) and t == 0):
                    act.wait_ge(s["kv_psum"], 8 * t - 3 + b)
                rows = slice(b * P, (b + 1) * P)
                copy(x_hi[:, :, rows], raw[:, :, rows]).then_inc(s["ctx_hi"], 1)

            def kv_copy(t, p, n):
                act.wait_ge(s["kv_psum"], 8 * t + n + 1)
                if n < 4:
                    if not (isinstance(t, int) and t == 0):
                        act.wait_ge(s["k1_low"], C * t)
                    nc.scalar.activation(k_t[:, n, :], ps[:, n % 2, :], ACT.Identity,
                                         bias=cols[:, 1, n:n + 1]).then_inc(s["kv_evac"], 1)
                else:
                    if not (isinstance(t, int) and t <= 1):
                        act.wait_ge(s["av_done"], 4 * (t - 1))
                    copy(v_buf[:, p, n - 4, :], ps[:, n % 2, :]).then_inc(s["kv_evac"], 1)

            def k_high(t, n):
                act.wait_ge(s["kv_evac"], 8 * t + n + 1)
                if n == 0 and not (isinstance(t, int) and t == 0):
                    act.wait_ge(s["k1_pack_in"], 144 * t)
                copy(k1_high[:, n, :], k_t[:, n, :]).then_inc(s["k1_high"], 1)

            def k_mid(t, n):
                act.wait_ge(s["k1_rest"], C * t + n + 1)
                copy(k1_parts[1][:, n, :], k_t[:, n, :]).then_inc(s["k1_mid"], 1)

            def s_copy(t, k, b, chunks=range(C)):
                for hg in chunks:
                    g = b * C + hg
                    if hg == 0 and not (isinstance(t, int) and B * t + b < RING):
                        act.wait_ge(s["av_done"], B * t + b + 1 - RING)
                    act.wait_ge(s["s_psum"], 16 * t + g + 1)
                    copy(scores(k, b)[:, hg * J:(hg + 1) * J, :], ps[:, 2 + g % 2, :]).then_inc(s["s_evac"], 1)

            def exp(t, k, b, mixed=False):
                if not (mixed and b == 3):
                    act.wait_ge(s["sub_done"], 4 * t + EXP_ORDER.index(b) + 1)
                part = scores(k, b)
                nc.scalar.activation(part, part, ACT.Exp).then_inc(s["exp_done"], 1)

            def first():
                ln_std(0)
                for c in range(C):
                    act.wait_ge(s["tr_done"], c + 1)
                    copy(x_t0[:, c, :], ps[:, 4 + c, :]).then_inc(s["x_hi_done"], 1)
                act.wait_ge(s["wk_in"], 16)
                copy(w_hi[:, 0], wk_raw).then_inc(s["wkv_hi"], 1)
                for b in range(B):
                    ctx_split(0, b)
                act.wait_ge(s["wv_in"], 16)
                copy(w_hi[:, 1], wv_raw).then_inc(s["wkv_hi"], 1)
                act.wait_ge(s["bq_done"], 1)
                act.wait_ge(s["wkv_lo"], 2)
                for hg in range(C):
                    act.wait_ge(s["q_psum"], hg + 1)
                    nc.scalar.activation(q1_float[:, hg, :], ps[:, 4 + hg, :], ACT.Identity,
                                         bias=bq_scaled[:, hg:hg + 1], scale=SCALE).then_inc(s["q1_float"], 1)
                    act.wait_ge(s["q1_float"], hg + 1)
                    copy(q1_parts[0][:, hg, :], q1_float[:, hg, :]).then_inc(s["q1_high"], 1)
                for hg in range(C):
                    act.wait_ge(s["q1_rest"], hg + 1)
                    copy(q1_parts[1][:, hg, :], q1_float[:, hg, :]).then_inc(s["q1_mid"], 1)
                act.wait_ge(s["cols_in"], 16)
                act.wait_ge(s["tab_steps"], 8)
                act.wait_ge(s["ln_done"], B)
                for n in range(8):
                    kv_copy(0, 0, n)
                    if n < C:
                        k_high(0, n)
                    if 1 <= n <= C:
                        k_mid(0, n - 1)
                    if n >= C:
                        ctx_split(1, n - C)
                s_copy(0, 0, 0, (0, 1))
                for n in range(C):
                    kv_copy(1, 1, n)
                    if n < 3:
                        s_copy(0, 0, (n + 1) // 2, (2, 3) if n % 2 == 0 else (0, 1))
                    k_high(1, n)
                k_mid(1, 0)
                s_copy(0, 0, 2)
                k_mid(1, 1)
                s_copy(0, 0, 3)
                k_mid(1, 2)
                k_mid(1, 3)

            def stage(t, k):
                more = not (isinstance(t, int) and t == T - 2)
                k1 = (k + 1) % 6
                for b in range(B):
                    kv_copy(t + 1, k1 % 2, C + b)
                    if more:
                        ctx_split(t + 2, b)
                    if b < 2:
                        exp(t, k, EXP_ORDER[b])
                if isinstance(t, int) and t == 0:
                    act.wait_ge(s["pos_done"], 1)
                s_copy(t + 1, k1, 0, (0, 1))
                exp(t, k, EXP_ORDER[2])
                exp(t, k, EXP_ORDER[3])
                for n in range(C):
                    if more:
                        kv_copy(t + 2, k % 2, n)
                    if n < 3:
                        s_copy(t + 1, k1, (n + 1) // 2, (2, 3) if n % 2 == 0 else (0, 1))
                    if more:
                        k_high(t + 2, n)
                if more:
                    k_mid(t + 2, 0)
                s_copy(t + 1, k1, 2)
                if more:
                    k_mid(t + 2, 1)
                s_copy(t + 1, k1, 3)
                if more:
                    k_mid(t + 2, 2)
                    k_mid(t + 2, 3)

            def last():
                weight_hi(0)
                for b in EXP_ORDER:
                    if b == 3:
                        act.wait_ge(s["sub_pool"], 1)
                    exp(T - 1, (T - 1) % 6, b, mixed=True)

            schedule(act, first, stage, last)

            def split_hi(c, bank):
                copy(x_hi[:, c, :], ps[:, bank, :]).then_inc(s["x_hi_done"], 1)

            for b in range(B):
                act.wait_ge(s["av_done"], B * (T - 1) + b + 1)
                split_hi(b, 4 + b)
            weight_hi(1)
            act.wait_ge(s["soft_a"], 1)
            nc.scalar.activation(soft[:, 1], soft[:, 0], ACT.Exp).then_inc(s["soft_b"], 1)
            act.wait_ge(s["soft_b"], 1)
            nc.scalar.activation(soft[:, 2], soft[:, 1], ACT.Ln, bias=1.0).then_inc(s["soft_c"], 1)

            ln_std(1)
            for c in range(C):
                act.wait_ge(s["tr_done"], C + c + 1)
                split_hi(c, 4 + c)
            weight_hi(2)
            for hg in range(C):
                act.wait_ge(s["q2_psum"], hg + 1)
                copy(k_t[:, hg, :], ps[:, hg, :]).then_inc(s["q2_evac"], 1)
                act.wait_ge(s["q2_evac"], hg + 1)
                copy(q_parts[:, 0, hg, :], k_t[:, hg, :]).then_inc(s["qh"], 1)
            for hg in range(C):
                act.wait_ge(s["qr"], hg + 1)
                copy(q_parts[:, 1, hg, :], q_rest[:, hg, :]).then_inc(s["qm"], 1)
            weight_hi(3)
            kf = v_buf[:, 0]
            for hg in range(C):
                act.wait_ge(s["k2_psum"], hg + 1)
                copy(kf[:, hg, :], ps[:, 4 + hg, :]).then_inc(s["kf_evac"], 1)
                act.wait_ge(s["kf_evac"], hg + 1)
                copy(k_parts[:, 0, hg, :], kf[:, hg, :]).then_inc(s["kh"], 1)
            for hg in range(C):
                act.wait_ge(s["kr"], hg + 1)
                copy(k_parts[:, 1, hg, :], kf[:, hg, :]).then_inc(s["km"], 1)
            weight_hi(4)
            for b in range(B):
                act.wait_ge(s["v2_psum"], b + 1)
                copy(v_buf[:, 1, b, :], ps[:, b, :]).then_inc(s["v2_evac"], 1)
            for n in range(16):
                act.wait_ge(s["rk_psum"], n + 1)
                copy(s_buf[:, 1, :, 8 * n:8 * n + 8].rearrange("p n l -> p l n"),
                     ps[:, n % 8, :].rearrange("p (l n) -> p l n", l=8)).then_inc(s["rk_evac"], 1)
            weight_hi(5)

            def exp2(b):
                if b >= SPLIT:
                    act.wait_ge(s["sub2"], b - SPLIT + 1)
                    part = lg[:, :, b, :]
                    nc.scalar.activation(part, part, ACT.Exp, scale=SCALE).then_inc(s["exp2"], 1)
                    return
                act.wait_ge(s["neg2"], b + 1)
                for n in range(H):
                    part = lg[:, n, b, :]
                    key = slice(b * H + n, b * H + n + 1)
                    nc.scalar.activation(part, part, ACT.Exp, bias=neg_max[:, key], scale=SCALE,
                                         accum_out=rsum[:, key]).then_inc(s["exp2"], 1)

            def at_copy(b):
                for hg in range(C):
                    act.wait_ge(s["at_psum"], C * b + hg + 1)
                    copy(probs_t[:, C * b + hg, :, :], ps[:, 4 + hg, :]).then_inc(s["at_done"], 1)

            exp2(0)
            exp2(1)
            exp2(2)
            act.wait_ge(s["lg_psum"], G)
            at_copy(0)
            at_copy(1)
            exp2(3)
            at_copy(2)
            at_copy(3)
            for b in range(B):
                act.wait_ge(s["av2"], b + 1)
                copy(k_t[:, b, :], ps[:, b, :]).then_inc(s["ot2_evac"], 1)
            act.wait_ge(s["ev2"], 4)
            ev_part = ps[:, 4:8, :].rearrange("p a n -> p (a n)").rearrange("p (q g j) -> p g q j", g=G, j=J)
            for i in (2, 3):
                for j in range(J):
                    copy(ev_half[j * HD:(j + 1) * HD, :, :, i - 2],
                         ev_part[i * HD:(i + 1) * HD, :, :, j]).then_inc(s["ev_copied"], 1)

            ln_std(2)
            for c in range(C):
                act.wait_ge(s["tr_done"], 2 * C + c + 1)
                split_hi(c, 4 + c)
            weight_hi(6)
            act.wait_ge(s["q3_bias"], B)
            nc.scalar.activation(s_buf[:, 1, 16:32, :], s_buf[:, 1, 0:16, :], ACT.Square).then_inc(s["q3_sq"], 1)
            act.wait_ge(s["q3_ss"], 1)
            nc.scalar.activation(rsum[:], rsum[:], ACT.Sqrt).then_inc(s["q3_rt"], 1)
            for hg in range(C):
                act.wait_ge(s["k3_psum"], hg + 1)
                for j in range(J // 2, J):
                    rows = slice(j * HD, (j + 1) * HD)
                    nc.scalar.activation(blocks[rows, hg::C, j, :], ps[rows, 4 + hg, :].rearrange("p (b q) -> p b q", b=B),
                                         ACT.Identity, bias=cols[rows, 2, hg:hg + 1]).then_inc(s["k3_blocks_act"], 1)
            weight_hi(7)
            act.wait_ge(s["q3t_psum"], 1)
            for c in range(C):
                copy(s_buf[:, 1, 32 + 4 * c:36 + 4 * c, :], ps[:, 4 + c, :]).then_inc(s["q3t_evac"], 1)

            def exp3(b):
                act.wait_ge(s["sub3"], b + 1)
                part = s_buf[:, 0, b * H:(b + 1) * H, :]
                nc.scalar.activation(part, part, ACT.Exp, scale=SCALE).then_inc(s["exp3"], 1)

            def at3_copy(b):
                for hg in range(C):
                    act.wait_ge(s["at3_psum"], C * b + hg + 1)
                    copy(probs_t[:, C * b + hg, :, :], ps[:, 4 * (b % 2) + hg, :]).then_inc(s["at3_done"], 1)

            exp3(0)
            exp3(1)
            exp3(2)
            act.wait_ge(s["lg3_psum"], G)
            at3_copy(0)
            exp3(3)
            for b in range(1, B):
                at3_copy(b)
            for b in range(B):
                act.wait_ge(s["av3"], b + 1)
                copy(k_t[:, b, :], ps[:, b, :]).then_inc(s["ot3_evac"], 1)
            for b in range(B):
                act.wait_ge(s["ot3_done"], b + 1)
                copy(x_hi[:, b, :], k_t[:, b, :]).then_inc(s["ot3_hi"], 1)
            act.wait_ge(s["g_sub"], 2)
            nc.scalar.activation(gate[:], gate[:], ACT.Exp).then_inc(s["g_exp"], 1)

        @block.gpsimd
        def _(pool):
            pool.memset(ident[:], 0.0).then_inc(s["ident_done"], 1)
            pool.wait_ge(s["ident_done"], 1)
            pool.affine_select(out=ident[:], in_=ident[:], compare_op=ALU.not_equal, fill=1.0, base=0,
                               pattern=[[-1, P]], channel_multiplier=1).then_inc(s["ident_done"], 1)

            pool.wait_ge(s["tab_in"], 32)
            for n, parts in enumerate((ek_parts, eq_parts)):
                t = tab_raw[:, n, 0:2 * P - 1]
                u, v, w = (parts[:, r, 0:2 * P - 1] for r in range(3))
                pool.tensor_copy(u, t).then_inc(s["tab_steps"], 1)
                pool.wait_ge(s["tab_steps"], 4 * n + 1)
                pool.tensor_tensor(t, t, u, ALU.subtract).then_inc(s["tab_steps"], 1)
                pool.wait_ge(s["tab_steps"], 4 * n + 2)
                pool.tensor_copy(v, t).then_inc(s["tab_steps"], 1)
                pool.wait_ge(s["tab_steps"], 4 * n + 3)
                pool.tensor_tensor(w, t, v, ALU.subtract).then_inc(s["tab_steps"], 1)
            pool.wait_ge(s["bv_in"], 16)

            def k_rest(t, n):
                pool.wait_ge(s["k1_high"], C * t + n + 1)
                pool.tensor_tensor(k_t[:, n, :], k_t[:, n, :], k1_high[:, n, :], ALU.subtract).then_inc(s["k1_rest"], 1)

            def k_low(t, n):
                pool.wait_ge(s["k1_mid"], C * t + n + 1)
                pool.tensor_tensor(k1_parts[2][:, n, :], k_t[:, n, :], k1_parts[1][:, n, :],
                                   ALU.subtract).then_inc(s["k1_low"], 1)

            def v_bias(t, p):
                for b in range(B):
                    pool.wait_ge(s["kv_evac"], 8 * t + 4 + b + 1)
                    pool.tensor_tensor(v_buf[:, p, b, :], v_buf[:, p, b, :], bv_all, ALU.add).then_inc(s["v_ready"], 1)

            def ctx_split(t):
                for b in range(B):
                    pool.wait_ge(s["ctx_hi"], B * t + b + 1)
                    rows = slice(b * P, (b + 1) * P)
                    pool.tensor_tensor(x_lo[:, :, rows], raw[:, :, rows], x_hi[:, :, rows],
                                       ALU.subtract).then_inc(s["ctx_lo"], 1)

            def weight_lo(n):
                pool.wait_ge(s["wsplit_hi"], n + 1)
                pool.tensor_tensor(w_lo[:, n % 2], raw[:], w_hi[:, n % 2], ALU.subtract).then_inc(s["wsplit_lo"], 1)

            def sum_first(t, k):
                pool.wait_ge(s["exp_done"], 4 * t + EXP_ORDER.index(0) + 1)
                acc = pool_tmp.rearrange("p (h q) -> p h q", q=P)
                part = scores(k, 0)
                pool.tensor_tensor(acc, part[:, 0:8], part[:, 8:16], ALU.add).then_inc(s["zadd"], 1)
                for n, w in enumerate((4, 2)):
                    pool.wait_ge(s["zadd"], 3 * t + n + 1)
                    pool.tensor_tensor(acc[:, 0:w], acc[:, 0:w], acc[:, w:2 * w], ALU.add).then_inc(s["zadd"], 1)
                pool.wait_ge(s["zadd"], 3 * t + 3)
                if not (isinstance(t, int) and t == 0):
                    pool.wait_ge(s["z_done"], t)
                pool.tensor_tensor(z_part[:, 0], acc[:, 0], acc[:, 1], ALU.add).then_inc(s["zpool"], 1)

            def normalise(t, k):
                pool.wait_ge(s["r_ready"], t + 1)
                part = scores(k, 3)
                r = r_all[:, :].rearrange("p (o q) -> p o q", o=1).broadcast_to([P, H, P])
                pool.tensor_tensor(part, part, r, ALU.mult).then_inc(s["attn_pool"], 1)

            def first():
                k_rest(0, 0)
                for n in range(C):
                    if n + 1 < C:
                        k_rest(0, n + 1)
                    k_low(0, n)
                ctx_split(1)
                v_bias(0, 0)
                for n in range(C):
                    k_rest(1, n)
                for n in range(C):
                    k_low(1, n)

            def stage(t, k):
                more = not (isinstance(t, int) and t == T - 2)
                if more:
                    ctx_split(t + 2)
                sum_first(t, k)
                if more:
                    for n in range(3):
                        k_rest(t + 2, n)
                normalise(t, k)
                if more:
                    k_rest(t + 2, 3)
                    for n in range(C):
                        k_low(t + 2, n)
                v_bias(t + 1, 1 - k % 2)

            def last():
                pool.wait_ge(s["m_ready"], T)
                part = scores((T - 1) % 6, 3)
                m = m_all[:, :].rearrange("p (o q) -> p o q", o=1).broadcast_to([P, H, P])
                pool.tensor_tensor(part, part, m, ALU.subtract).then_inc(s["sub_pool"], 1)
                sum_first(T - 1, (T - 1) % 6)
                weight_lo(0)
                normalise(T - 1, (T - 1) % 6)
                pool.wait_ge(s["x_in"], 32)
                pool.wait_ge(s["bo_in"], 16)
                bo = bo_all.rearrange("p (o e) -> p o e", o=1).broadcast_to([P, B, D])
                pool.tensor_tensor(x_res[:], x_res[:], bo, ALU.add).then_inc(s["xb_done"], 1)
                pool.wait_ge(s["s_psum"], 16 * T)
                pool.memset(blocks[:], 0.0).then_inc(s["qzero"], 1)

            schedule(pool, first, stage, last)

            for n in range(1, 6):
                weight_lo(n)
            pool.wait_ge(s["ln_done"], 3 * B)
            pool.wait_ge(s["b3_in"], 16)
            bp = bias3[:, 3:4, :].broadcast_to([P, B, D])
            pool.tensor_tensor(x_res[:], x_res[:], bp, ALU.add).then_inc(s["xp_done"], 1)
            pool.wait_ge(s["soft_d"], 1)
            qe = bias3[:, 1, :].rearrange("p (h d) -> p h d", h=H)
            pool.tensor_tensor(qe, qe, soft[:, 0, :].rearrange("p (h o) -> p h o", o=1).broadcast_to([P, H, HD]),
                               ALU.mult).then_inc(s["qe_done"], 1)
            weight_lo(6)
            weight_lo(7)

        @block.vector
        def _(dve):
            tt = nc.vector.tensor_tensor

            def layer_norm(k, ready):
                for b in range(B):
                    ready(b)
                    nc.vector.bn_stats(stats[:, b, :], x_res[:, b, :]).then_inc(s["stats_done"], 1)
                for b in range(B):
                    dve.wait_ge(s["stats_done"], B * k + b + 1)
                    nc.vector.bn_aggr(mean_var[:, b, :], stats[:, b, :]).then_inc(s["mv_done"], 1)
                dve.wait_ge(s["mv_done"], B * (k + 1))
                nc.vector.tensor_scalar(rstd[:], mean_var[:, :, 1], EPS, None, ALU.add).then_inc(s["var_done"], 1)
                dve.wait_ge(s["std_done"], k + 1)
                nc.vector.reciprocal(rstd[:], rstd[:]).then_inc(s["rstd_done"], 1)
                dve.wait_ge(s["rstd_done"], k + 1)
                for b in range(B):
                    y = y_ln0 if k == 0 else y_ln
                    nc.vector.tensor_scalar(y[:, b, :], x_res[:, b, :], mean_var[:, b, 0:1], rstd[:, b:b + 1],
                                            ALU.subtract, ALU.mult).then_inc(s["ln_done"], 1)

            dve.wait_ge(s["x_in"], 16)
            layer_norm(0, lambda b: None)
            dve.wait_ge(s["cols_in"], 16)
            nc.vector.tensor_scalar(bq_scaled[:], cols[:, 0, :], SCALE, None, ALU.mult).then_inc(s["bq_done"], 1)
            dve.wait_ge(s["wkv_hi"], 1)
            tt(w_lo[:, 0], wk_raw, w_hi[:, 0], ALU.subtract).then_inc(s["wkv_lo"], 1)
            for b in range(B):
                dve.wait_ge(s["ctx_hi"], b + 1)
                rows = slice(b * P, (b + 1) * P)
                tt(x_lo[:, :, rows], raw[:, :, rows], x_hi[:, :, rows], ALU.subtract).then_inc(s["ctx_lo"], 1)
            dve.wait_ge(s["wkv_hi"], 2)
            tt(w_lo[:, 1], wv_raw, w_hi[:, 1], ALU.subtract).then_inc(s["wkv_lo"], 1)
            for hg in range(C):
                dve.wait_ge(s["q1_high"], hg + 1)
                tt(q1_float[:, hg, :], q1_float[:, hg, :], q1_parts[0][:, hg, :], ALU.subtract).then_inc(s["q1_rest"], 1)
            for hg in range(C):
                dve.wait_ge(s["q1_mid"], hg + 1)
                tt(q1_parts[2][:, hg, :], q1_float[:, hg, :], q1_parts[1][:, hg, :], ALU.subtract).then_inc(s["q1_low"], 1)
            dve.wait_ge(s["rel_in"], 32)
            tt(eq_rel, eq_rel, ek_rel, ALU.mult).then_inc(s["pos_mul"], 1)
            dve.wait_ge(s["pos_mul"], 1)
            nc.vector.tensor_reduce(pos[:], eq_rel, AX.X, ALU.add).then_inc(s["pos_done"], 1)
            dve.wait_ge(s["small_in"], 48)
            nc.vector.scalar_tensor_tensor(soft[:, 0], temp[:], -1.0, temp[:], ALU.mult, ALU.min).then_inc(s["soft_a"], 1)

            def over_heads(t):
                return t[:, :].rearrange("p (o q) -> p o q", o=1).broadcast_to([P, H, P])

            def maxima(t, k):
                for b in range(B):
                    dve.wait_ge(s["s_evac"], 16 * t + 4 * b + 4)
                    nc.vector.tensor_reduce(m_part[:, b, :], scores(k, b).rearrange("p h q -> p q h"),
                                            AX.X, ALU.max).then_inc(s["max_done"], 1)
                dve.wait_ge(s["max_done"], 4 * t + 4)
                nc.vector.tensor_reduce(m_all[:], m_part[:, :, :].rearrange("p b q -> p q b"), AX.X,
                                        ALU.max).then_inc(s["m_ready"], 1)

            def softmax(t, k, order=EXP_ORDER):
                dve.wait_ge(s["m_ready"], t + 1)
                for b in order:
                    part = scores(k, b)
                    tt(part, part, over_heads(m_all), ALU.subtract).then_inc(s["sub_done"], 1)
                for b in range(1, B):
                    dve.wait_ge(s["exp_done"], 4 * t + EXP_ORDER.index(b) + 1)
                    nc.vector.tensor_reduce(z_part[:, b, :], scores(k, b).rearrange("p h q -> p q h"),
                                            AX.X, ALU.add).then_inc(s["sum_dve"], 1)
                dve.wait_ge(s["sum_dve"], 3 * t + 3)
                dve.wait_ge(s["zpool"], t + 1)
                nc.vector.tensor_reduce(z_all[:], z_part.rearrange("p b q -> p q b"), AX.X,
                                        ALU.add).then_inc(s["z_done"], 1)
                dve.wait_ge(s["z_done"], t + 1)
                if not (isinstance(t, int) and t == 0):
                    dve.wait_ge(s["attn_pool"], t)
                nc.vector.reciprocal(r_all[:], z_all[:]).then_inc(s["r_ready"], 1)
                dve.wait_ge(s["r_ready"], t + 1)
                for b in range(3):
                    part = scores(k, b)
                    tt(part, part, over_heads(r_all), ALU.mult).then_inc(s["attn_dve"], 1)

            def first():
                maxima(0, 0)

            def stage(t, k):
                softmax(t, k)
                maxima(t + 1, (k + 1) % 6)

            def last():
                softmax(T - 1, (T - 1) % 6, EXP_ORDER[:3])

            schedule(dve, first, stage, last)

            def split_lo(c, bank, n):
                dve.wait_ge(s["x_hi_done"], C * n + c + 1)
                tt(x_lo[:, c, :], ps[:, bank, :], x_hi[:, c, :], ALU.subtract).then_inc(s["x_lo_done"], 1)

            for b in range(B):
                split_lo(b, 4 + b, 1)
            dve.wait_ge(s["xb_done"], 1)
            def residual1(b):
                dve.wait_ge(s["wo_psum"], b + 1)
                tt(x_res[:, b, :], ps[:, b, :], x_res[:, b, :], ALU.add).then_inc(s["x1_done"], 1)
                dve.wait_ge(s["x1_done"], b + 1)

            layer_norm(1, residual1)
            dve.wait_ge(s["soft_c"], 1)
            nc.vector.scalar_tensor_tensor(soft[:, 0], temp[:], 0.0, soft[:, 2], ALU.max, ALU.add).then_inc(s["soft_d"], 1)
            for c in range(C):
                split_lo(c, 4 + c, 2)
            for hg in range(C):
                dve.wait_ge(s["qh"], hg + 1)
                tt(q_rest[:, hg, :], k_t[:, hg, :], q_parts[:, 0, hg, :], ALU.subtract).then_inc(s["qr"], 1)
            for hg in range(C):
                dve.wait_ge(s["qm"], hg + 1)
                tt(q_parts[:, 2, hg, :], q_rest[:, hg, :], q_parts[:, 1, hg, :], ALU.subtract).then_inc(s["ql"], 1)
            dve.wait_ge(s["qzero"], 1)
            kf = v_buf[:, 0]
            for hg in range(C):
                dve.wait_ge(s["kf_evac"], hg + 1)
                for j in range(J):
                    rows = slice(j * HD, (j + 1) * HD)
                    nc.vector.tensor_copy(blocks[rows, hg::C, j, :],
                                          kf[rows, hg, :].rearrange("p (b q) -> p b q", b=B)).then_inc(s["k2_blocks"], 1)
                dve.wait_ge(s["kh"], hg + 1)
                dve.wait_ge(s["k2_blocks"], 4 * hg + 4)
                tt(kf[:, hg, :], kf[:, hg, :], k_parts[:, 0, hg, :], ALU.subtract).then_inc(s["kr"], 1)
            for hg in range(C):
                dve.wait_ge(s["km"], hg + 1)
                tt(k_parts[:, 2, hg, :], kf[:, hg, :], k_parts[:, 1, hg, :], ALU.subtract).then_inc(s["kl"], 1)
            dve.wait_ge(s["pos_done"], 1)
            dve.wait_ge(s["attn_dve"], 3 * T)
            for n in range(16):
                dve.wait_ge(s["rq_psum"], n + 1)
                pm = pos[:, 8 * n:8 * n + 8].rearrange("p (m o) -> p m o", o=1).broadcast_to([P, 8, B * H])
                tt(s_buf[:, 0, :, 8 * n:8 * n + 8].rearrange("p n m -> p m n"),
                   ps[:, n % 8, :].rearrange("p (m n) -> p m n", m=8), pm, ALU.add).then_inc(s["rq_evac"], 1)
            dve.wait_ge(s["rq_evac"], 16)

            def keys(t, b):
                return t[:, b * H:(b + 1) * H].rearrange("p (h o) -> p h o", o=1).broadcast_to([P, H, P])

            lg4 = s_buf[:, 0].rearrange("p (j c b) q -> p j c b q", j=J, c=C)
            for b in range(B):
                for hg in range(C):
                    g = b * C + hg
                    dve.wait_ge(s["lg_psum"], g + 1)
                    part = lg4[:, :, hg, b, :]
                    tt(part, ps[:, hg, :].rearrange("p (j m) -> p j m", j=J), part, ALU.add).then_inc(s["lg_done"], 1)
                dve.wait_ge(s["lg_done"], C * (b + 1))
                part = lg[:, :, b, :]
                nc.vector.tensor_reduce(rmax[:, b * H:(b + 1) * H], part, AX.X, ALU.max).then_inc(s["max2"], 1)
                dve.wait_ge(s["max2"], b + 1)
                if b < SPLIT:
                    nc.vector.tensor_scalar(neg_max[:, b * H:(b + 1) * H], rmax[:, b * H:(b + 1) * H], -SCALE, None,
                                            ALU.mult).then_inc(s["neg2"], 1)
                else:
                    tt(part, part, keys(rmax, b), ALU.subtract).then_inc(s["sub2"], 1)
            for b in range(SPLIT, B):
                dve.wait_ge(s["exp2"], exp2_count(b))
                nc.vector.tensor_reduce(rsum[:, b * H:(b + 1) * H], lg[:, :, b, :], AX.X, ALU.add).then_inc(s["sum2"], 1)
            dve.wait_ge(s["sum2"], B - SPLIT)
            nc.vector.reciprocal(rinv[:], rsum[:]).then_inc(s["rinv2"], 1)
            dve.wait_ge(s["ot2_evac"], B)
            dve.wait_ge(s["ev2"], 4)
            ev_part = ps[:, 4:8, :].rearrange("p a n -> p (a n)").rearrange("p (q g j) -> p g q j", g=G, j=J)
            out_t = k_t[:, :, :].rearrange("p b (c q i) -> p (b c) q i", c=C, i=4)
            for i in range(2):
                for j in range(J):
                    dst = out_t[j * HD:(j + 1) * HD, :, :, i]
                    tt(dst, ev_part[i * HD:(i + 1) * HD, :, :, j], dst, ALU.add).then_inc(s["ot2_done"], 1)
            dve.wait_ge(s["ev_copied"], 8)
            dst = out_t[:, :, :, 2:4]
            tt(dst, ev_half, dst, ALU.add).then_inc(s["ot2_done"], 1)
            dve.wait_ge(s["rinv2"], 1)
            for b in range(B):
                dve.wait_ge(s["back_psum"], b + 1)
                r = rinv[:, b * H:(b + 1) * H].rearrange("p (j c o) -> p c j o", j=J, o=1).broadcast_to([P, C, J, HD])
                tt(v_buf[:, 0, b, :].rearrange("p (c j d) -> p c j d", c=C, j=J),
                   ps[:, b, :].rearrange("p (c j d) -> p c j d", c=C, j=J), r, ALU.mult).then_inc(s["back_mul"], 1)

            def residual2(b):
                dve.wait_ge(s["back_mul"], b + 1)
                tt(x_res[:, b, :], x_res[:, b, :], v_buf[:, 0, b, :], ALU.add).then_inc(s["x2_done"], 1)
                dve.wait_ge(s["x2_done"], b + 1)

            layer_norm(2, residual2)
            for c in range(C):
                split_lo(c, 4 + c, 3)

            dve.wait_ge(s["b3_in"], 16)
            q3 = s_buf[:, 1, 0:16, :].rearrange("p (b a) n -> p b (a n)", b=B)
            q3h = s_buf[:, 1, 0:16, :].rearrange("p a n -> p (a n)").rearrange("p (n d) -> p n d", d=HD)
            sq = s_buf[:, 1, 16:32, :].rearrange("p a n -> p (a n)").rearrange("p (n d) -> p n d", d=HD)
            for b in range(B):
                dve.wait_ge(s["q3_psum"], b + 1)
                tt(q3[:, b, :], ps[:, b, :], bias3[:, 0, :], ALU.add).then_inc(s["q3_bias"], 1)
            dve.wait_ge(s["q3_sq"], 1)
            nc.vector.tensor_reduce(rsum[:], sq, AX.X, ALU.add).then_inc(s["q3_ss"], 1)
            dve.wait_ge(s["q3_rt"], 1)
            nc.vector.reciprocal(rinv[:], rsum[:]).then_inc(s["q3_rn"], 1)
            dve.wait_ge(s["q3_rn"], 1)
            r = rinv[:, :].rearrange("p (b h) -> p b h", b=B)
            tt(r, r, soft[:, 0:1, :].broadcast_to([P, B, H]), ALU.mult).then_inc(s["q3_rsp"], 1)
            for hg in range(C):
                dve.wait_ge(s["k3_psum"], hg + 1)
                for j in range(J // 2):
                    rows = slice(j * HD, (j + 1) * HD)
                    nc.vector.tensor_scalar(blocks[rows, hg::C, j, :],
                                            ps[rows, 4 + hg, :].rearrange("p (b q) -> p b q", b=B),
                                            cols[rows, 2, hg:hg + 1], None, ALU.add).then_inc(s["k3_blocks"], 1)
            dve.wait_ge(s["q3_rsp"], 1)
            dve.wait_ge(s["qe_done"], 1)
            for b in range(B):
                dst = q3h[:, b * H:(b + 1) * H, :]
                tt(dst, dst, rinv[:, b * H:(b + 1) * H].rearrange("p (h o) -> p h o", o=1).broadcast_to([P, H, HD]),
                   ALU.mult).then_inc(s["q3_a"], 1)
                dve.wait_ge(s["q3_a"], b + 1)
                tt(q3[:, b, :], q3[:, b, :], bias3[:, 1, :], ALU.add).then_inc(s["q3_done"], 1)
            for b in range(B):
                dve.wait_ge(s["v3_psum"], b + 1)
                tt(v_buf[:, 1, b, :], ps[:, b, :], bias3[:, 2, :], ALU.add).then_inc(s["v3_done"], 1)
            for b in range(B):
                dve.wait_ge(s["lg3_psum"], C * (b + 1))
                bank = 4 * (b % 2)
                part = ps[:, bank:bank + 4, :].rearrange("p a n -> p (a n)").rearrange("p (h m) -> p h m", m=P)
                nc.vector.tensor_reduce(rmax[:, b * H:(b + 1) * H], part, AX.X, ALU.max).then_inc(s["max3"], 1)
                dve.wait_ge(s["max3"], b + 1)
                tt(s_buf[:, 0, b * H:(b + 1) * H, :], part, keys(rmax, b), ALU.subtract).then_inc(s["sub3"], 1)
            for b in range(B):
                dve.wait_ge(s["exp3"], b + 1)
                nc.vector.tensor_reduce(rsum[:, b * H:(b + 1) * H], s_buf[:, 0, b * H:(b + 1) * H, :], AX.X,
                                        ALU.add).then_inc(s["sum3"], 1)
                dve.wait_ge(s["sum3"], b + 1)
                nc.vector.reciprocal(rinv[:, b * H:(b + 1) * H], rsum[:, b * H:(b + 1) * H]).then_inc(s["rinv3"], 1)
                dve.wait_ge(s["rinv3"], b + 1)
                nc.vector.tensor_copy(v_buf[:, 0, b, :].rearrange("p (h d) -> p h d", h=H),
                                      rinv[:, b * H:(b + 1) * H].rearrange("p (h o) -> p h o", o=1)
                                      .broadcast_to([P, H, HD])).then_inc(s["rexp3"], 1)
            for b in range(B):
                dve.wait_ge(s["ot3_evac"], b + 1)
                dve.wait_ge(s["rb_psum"], b + 1)
                tt(k_t[:, b, :], k_t[:, b, :], ps[:, 4 + b, :], ALU.mult).then_inc(s["ot3_done"], 1)
            for b in range(B):
                dve.wait_ge(s["ot3_hi"], b + 1)
                tt(x_lo[:, b, :], k_t[:, b, :], x_hi[:, b, :], ALU.subtract).then_inc(s["ot3_lo"], 1)
            for b in range(B):
                dve.wait_ge(s["g_psum"], b + 1)
                tt(gate[:, b, :], ps[:, 4 + b, 0:NG], b_gate[:], ALU.add).then_inc(s["g_bias"], 1)
            dve.wait_ge(s["g_bias"], B)
            routed, shared = gate[:, :, 0:NR], gate[:, :, NR:NG]
            nc.vector.tensor_reduce(gtmp[:, :, 0], routed, AX.X, ALU.max).then_inc(s["g_max"], 1)
            nc.vector.tensor_reduce(gtmp[:, :, 1], shared, AX.X, ALU.max).then_inc(s["g_max"], 1)
            dve.wait_ge(s["g_max"], 2)
            tt(routed, routed, gtmp[:, :, 0:1].broadcast_to([P, B, NR]), ALU.subtract).then_inc(s["g_sub"], 1)
            tt(shared, shared, gtmp[:, :, 1:2].broadcast_to([P, B, 2]), ALU.subtract).then_inc(s["g_sub"], 1)
            dve.wait_ge(s["g_exp"], 1)
            for b in range(B):
                nc.vector.max(top8[:, b, :], gate[:, b, 0:NR]).then_inc(s["g_top"], 1)
            nc.vector.tensor_reduce(gtmp[:, :, 2], routed, AX.X, ALU.add).then_inc(s["g_steps"], 1)
            nc.vector.tensor_reduce(gtmp[:, :, 3], shared, AX.X, ALU.add).then_inc(s["g_steps"], 1)
            dve.wait_ge(s["g_top"], B)
            nc.vector.tensor_reduce(gtmp[:, :, 4], top8[:, :, 0:3], AX.X, ALU.add).then_inc(s["g_steps"], 1)
            dve.wait_ge(s["g_steps"], 3)
            nc.vector.reciprocal(gtmp[:, :, 2:4], gtmp[:, :, 2:4]).then_inc(s["g_steps"], 1)
            dve.wait_ge(s["g_steps"], 4)
            tt(shared, shared, gtmp[:, :, 3:4].broadcast_to([P, B, 2]), ALU.mult).then_inc(s["g_steps"], 1)
            nc.vector.scalar_tensor_tensor(gtmp[:, :, 4], gtmp[:, :, 4], 3.0, gtmp[:, :, 2], ALU.mult,
                                           ALU.mult).then_inc(s["g_steps"], 1)
            dve.wait_ge(s["g_steps"], 6)
            tt(gtmp[:, :, 5], gate[:, :, NR], gate[:, :, NR + 1], ALU.add).then_inc(s["g_steps"], 1)
            nc.vector.scalar_tensor_tensor(gtmp[:, :, 6], gate[:, :, NR + 1], 2.0, gtmp[:, :, 4], ALU.mult,
                                           ALU.mult).then_inc(s["g_steps"], 1)
            dve.wait_ge(s["g_steps"], 8)
            nc.vector.scalar_tensor_tensor(gtmp[:, :, 7], gate[:, :, NR], 2.0, gtmp[:, :, 5], ALU.mult,
                                           ALU.mult).then_inc(s["g_steps"], 1)
            dve.wait_ge(s["g_steps"], 9)
            tt(rstd[:], gtmp[:, :, 6], gtmp[:, :, 7], ALU.add).then_inc(s["g_steps"], 1)
            dve.wait_ge(s["g_steps"], 10)
            dve.wait_ge(s["xp_done"], 1)
            for b in range(B):
                dve.wait_ge(s["y_psum"], b + 1)
                nc.vector.scalar_tensor_tensor(x_res[:, b, :], ps[:, b, :], rstd[:, b:b + 1], x_res[:, b, :],
                                               ALU.mult, ALU.add).then_inc(s["fin_done"], 1)


def kernel(**inputs):
    import concourse.bacc as bacc
    from concourse.bass_utils import run_bass_kernel_spmd

    f = {k: np.asarray(v) for k, v in inputs.items()}

    def chunks(w):
        return w.reshape(C, P, -1).transpose(1, 0, 2)

    rel = np.clip(np.arange(P)[:, None] - np.arange(P)[None, :], -64, 64) + 64
    span = np.arange(2 * P - 1)
    arrays = {
        "x": f["x"],
        "ctxT": f["ctx_1024"].reshape(B, T, P, C, P).transpose(1, 4, 3, 0, 2).reshape(T, P, C, D),
        "Wq1": chunks(f["L0_xattn_Wq"]), "Wk1": chunks(f["L0_xattn_Wk"]), "Wv1": chunks(f["L0_xattn_Wv"]),
        "Wo1": chunks(f["L0_xattn_Wo"]), "bv1": f["L0_xattn_bv"], "bo1": f["L0_xattn_bo"],
        "cols": np.stack([f["L0_xattn_bq"], f["L0_xattn_bk"], f["L0_ffn_bk"]]).reshape(3, C, P).transpose(2, 0, 1),
        "Wq2": chunks(f["L0_attn_Wq"]), "Wk2": chunks(f["L0_attn_Wk"]), "Wv2": chunks(f["L0_attn_Wv"]),
        "EqRel": f["L0_attn_Eq"][rel], "EkRel": f["L0_attn_Ek"][rel],
        "EvRel": f["L0_attn_Ev"][rel.T],
        "EkTab": np.tile(f["L0_attn_Ek"][np.clip(127 - span, -64, 64) + 64].T, (3, 1)),
        "EqTab": np.tile(f["L0_attn_Eq"][np.clip(span - 127, -64, 64) + 64].T, (3, 1)),
        "Wq3": chunks(f["L0_ffn_Wq"].T), "Wk3": chunks(f["L0_ffn_Wk"].T), "Wv3": chunks(f["L0_ffn_Wv"].T),
        "Wp3": chunks(f["L0_ffn_Wp"].T),
        "Wg": chunks(np.concatenate([f["L0_ffn_Wr"], f["L0_ffn_Ws"]]).T),
        "bg": np.concatenate([f["L0_ffn_br"], f["L0_ffn_bs"]]),
        "temp": f["L0_ffn_temperature"].reshape(H),
        "bias3": np.stack([f["L0_ffn_bq"], f["L0_ffn_query_embedding"].reshape(D), f["L0_ffn_bv"], f["L0_ffn_bp"]]),
    }
    arrays = {k: np.ascontiguousarray(v) for k, v in arrays.items()}
    nc = bacc.Bacc("TRN2", target_bir_lowering=False, num_devices=1)
    aps = {k: nc.dram_tensor("in_" + k, v.shape, mybir.dt.from_np(v.dtype), kind="ExternalInput").ap()
           for k, v in arrays.items()}
    out = nc.dram_tensor("out", (B, P, D), F32, kind="ExternalOutput").ap()
    program(nc, aps, out)
    r = run_bass_kernel_spmd(nc, [{"in_" + k: v for k, v in arrays.items()}], core_ids=[0])
    return r.results[0]["out"]
```
